# Optimizing a Trainium2 kernel written in Bass

```python
import numpy as np
import jax
import jax.numpy as jnp

def _softmax(x, axis=-1):
    return jax.nn.softmax(x, axis=axis)

def _gelu(x):
    return jax.nn.gelu(x, approximate=True)

def _silu(x):
    return jax.nn.silu(x)

def _sigmoid(x):
    return jax.nn.sigmoid(x)

def _layernorm(x, axis=-1, eps=1e-05):
    m = jnp.mean(x, axis=axis, keepdims=True)
    v = jnp.var(x, axis=axis, keepdims=True)
    return (x - m) / jnp.sqrt(v + eps)

def _scatter_add(tgt, idx, src, axis=0):
    return tgt.at[idx].add(src)

def _segment_sum(src, seg, n):
    return jax.ops.segment_sum(src, seg, n)
kernel_name = 'mk_gnn_resnorm_d2_gnn_r8_bca2d2'

def setup_inputs(seed: int=0):
    np.random.seed(seed)
    _w = jnp.asarray

    def _rec_inputs():
        import jax
        import jax.numpy as jnp
        _gk = jax.random.key(seed)
        x = 8.953e-05 + 1 * jax.random.normal(jax.random.fold_in(_gk, 1), (12500, 64), jnp.float32)
        src = jax.random.randint(jax.random.fold_in(_gk, 2), (200000,), 0, 12500, jnp.int32)
        dst = jax.random.randint(jax.random.fold_in(_gk, 3), (200000,), 0, 12500, jnp.int32)
        _o = jnp.argsort(dst, stable=True)
        src = src[_o]
        dst = dst[_o]
        edge_attr_64 = 1.36993e-05 + 0.999972 * jax.random.normal(jax.random.fold_in(_gk, 11), (200000, 64), jnp.float32)
        edge_attr_9 = 0.000739051 + 0.999958 * jax.random.normal(jax.random.fold_in(_gk, 12), (200000, 9), jnp.float32)
        return (x, src, dst, edge_attr_64, edge_attr_9)
    x, src, dst, edge_attr_64, edge_attr_9 = _rec_inputs()

    def _L0_gnn_setup():
        import jax, jax.numpy as jnp
        import numpy as np
        N, E = (1250, 40000)
        D, S, HE = (64, 9, 64)
        H, DQK, DV = (8, 16, 16)
        OK, OV = (H * DQK, H * DV)
        EPS_BN = 1e-05

        def tensor_product(x_e, sh, w, C):
            acc = sh[:, 0:1] * (x_e @ C[:, 0, :])
            for s in range(1, S):
                acc = acc + sh[:, s:s + 1] * (x_e @ C[:, s, :])
            return acc * w

        def mlp2(x, w1, b1, w2, b2):
            return jax.nn.relu(x @ w1 + b1) @ w2 + b2
        key = jax.random.key(seed)
        ks = jax.random.split(key, 20)
        g = lambda k, shape, fan: jax.random.normal(k, shape, jnp.float32) / np.float32(np.sqrt(fan))
        return {'tfn_features': jax.random.normal(ks[0], (N, D), jnp.float32), 'edge_features': jax.random.normal(ks[1], (E, HE), jnp.float32), 'edge_sh': jax.random.normal(ks[2], (E, S), jnp.float32), 'Wq': g(ks[3], (D, OK), D), 'Cqk': g(ks[4], (D, S, OK), D * S), 'Cv': g(ks[5], (D, S, OV), D * S), 'k_w1': g(ks[6], (HE, HE), HE), 'k_b1': jnp.zeros((HE,), jnp.float32), 'k_w2': g(ks[7], (HE, OK), HE), 'k_b2': jnp.zeros((OK,), jnp.float32), 'v_w1': g(ks[8], (HE, HE), HE), 'v_b1': jnp.zeros((HE,), jnp.float32), 'v_w2': g(ks[9], (HE, OV), HE), 'v_b2': jnp.zeros((OV,), jnp.float32), 'W_out': g(ks[10], (OV, D), OV), 'W_self': g(ks[11], (D, D), D), 'gamma': jnp.ones((D,), jnp.float32), 'beta': jnp.zeros((D,), jnp.float32), 'edge_index': jax.random.randint(ks[12], (2, E), 0, N, dtype=jnp.int32)}
    _L0_gnn_all = _L0_gnn_setup()
    _L0_gnn_in = {k: v for k, v in _L0_gnn_all.items() if k in ('Wq', 'Cqk', 'Cv', 'k_w1', 'k_b1', 'k_w2', 'k_b2', 'v_w1', 'v_b1', 'v_w2', 'v_b2', 'W_out', 'W_self', 'gamma', 'beta')}
    del _L0_gnn_all

    def _L1_gnn_setup():
        import jax, jax.numpy as jnp
        import numpy as np
        N_NODES = 6250
        N_EDGES = 100000
        H_DIM = 64

        def scatter_mean(e, receiver, num_segments):
            sums = jax.ops.segment_sum(e, receiver, num_segments=num_segments)
            counts = jax.ops.segment_sum(jnp.ones((e.shape[0],), e.dtype), receiver, num_segments=num_segments)
            return sums / jnp.maximum(counts, 1.0)[:, None]
        key = jax.random.key(seed)
        ks = jax.random.split(key, 10)
        h = H_DIM
        v = jax.random.normal(ks[0], (N_NODES, h), dtype=jnp.float32)
        e = jax.random.normal(ks[1], (N_EDGES, h), dtype=jnp.float32)
        edge_index = jax.random.randint(ks[2], (2, N_EDGES), 0, N_NODES, dtype=jnp.int64)

        def glorot(k, shape):
            fan_in, fan_out = shape
            lim = np.sqrt(6.0 / (fan_in + fan_out)).astype(np.float32)
            return jax.random.uniform(k, shape, jnp.float32, -lim, lim)
        W0 = glorot(ks[3], (2 * h, h))
        b0 = jnp.zeros((h,), jnp.float32)
        W1 = glorot(ks[4], (h, h))
        b1 = jnp.zeros((h,), jnp.float32)
        W2 = glorot(ks[5], (h, h))
        b2 = jnp.zeros((h,), jnp.float32)
        return {'v': v, 'edge_index': edge_index, 'e': e, 'W0': W0, 'b0': b0, 'W1': W1, 'b1': b1, 'W2': W2, 'b2': b2}
    _L1_gnn_all = _L1_gnn_setup()
    _L1_gnn_in = {k: v for k, v in _L1_gnn_all.items() if k in ('W0', 'b0', 'W1', 'b1', 'W2', 'b2')}
    del _L1_gnn_all
    return {'x': x, 'src': src, 'dst': dst, 'edge_attr_64': edge_attr_64, 'edge_attr_9': edge_attr_9, 'L0_gnn_Wq': _L0_gnn_in['Wq'], 'L0_gnn_Cqk': _L0_gnn_in['Cqk'], 'L0_gnn_Cv': _L0_gnn_in['Cv'], 'L0_gnn_k_w1': _L0_gnn_in['k_w1'], 'L0_gnn_k_b1': _L0_gnn_in['k_b1'], 'L0_gnn_k_w2': _L0_gnn_in['k_w2'], 'L0_gnn_k_b2': _L0_gnn_in['k_b2'], 'L0_gnn_v_w1': _L0_gnn_in['v_w1'], 'L0_gnn_v_b1': _L0_gnn_in['v_b1'], 'L0_gnn_v_w2': _L0_gnn_in['v_w2'], 'L0_gnn_v_b2': _L0_gnn_in['v_b2'], 'L0_gnn_W_out': _L0_gnn_in['W_out'], 'L0_gnn_W_self': _L0_gnn_in['W_self'], 'L0_gnn_gamma': _L0_gnn_in['gamma'], 'L0_gnn_beta': _L0_gnn_in['beta'], 'L1_gnn_W0': _L1_gnn_in['W0'], 'L1_gnn_b0': _L1_gnn_in['b0'], 'L1_gnn_W1': _L1_gnn_in['W1'], 'L1_gnn_b1': _L1_gnn_in['b1'], 'L1_gnn_W2': _L1_gnn_in['W2'], 'L1_gnn_b2': _L1_gnn_in['b2']}

def reference(x, src, dst, edge_attr_64, edge_attr_9, L0_gnn_Wq, L0_gnn_Cqk, L0_gnn_Cv, L0_gnn_k_w1, L0_gnn_k_b1, L0_gnn_k_w2, L0_gnn_k_b2, L0_gnn_v_w1, L0_gnn_v_b1, L0_gnn_v_w2, L0_gnn_v_b2, L0_gnn_W_out, L0_gnn_W_self, L0_gnn_gamma, L0_gnn_beta, L1_gnn_W0, L1_gnn_b0, L1_gnn_W1, L1_gnn_b1, L1_gnn_W2, L1_gnn_b2):
    import jax
    import jax.numpy as jnp

    def _L0_gnn_ref(tfn_features, edge_features, edge_sh, Wq, Cqk, Cv, k_w1, k_b1, k_w2, k_b2, v_w1, v_b1, v_w2, v_b2, W_out, W_self, gamma, beta, edge_index):
        import jax, jax.numpy as jnp
        import numpy as np
        N, E = (1250, 40000)
        D, S, HE = (64, 9, 64)
        H, DQK, DV = (8, 16, 16)
        OK, OV = (H * DQK, H * DV)
        EPS_BN = 1e-05

        def tensor_product(x_e, sh, w, C):
            acc = sh[:, 0:1] * (x_e @ C[:, 0, :])
            for s in range(1, S):
                acc = acc + sh[:, s:s + 1] * (x_e @ C[:, s, :])
            return acc * w

        def mlp2(x, w1, b1, w2, b2):
            return jax.nn.relu(x @ w1 + b1) @ w2 + b2
        edge_dst, edge_src = (edge_index[0], edge_index[1])
        n = tfn_features.shape[0]
        q = (tfn_features @ Wq).reshape(n, H, DQK)
        x_dst = tfn_features[edge_dst]
        wk = mlp2(edge_features, k_w1, k_b1, k_w2, k_b2)
        wv = mlp2(edge_features, v_w1, v_b1, v_w2, v_b2)
        k = tensor_product(x_dst, edge_sh, wk, Cqk).reshape(-1, H, DQK)
        v = tensor_product(x_dst, edge_sh, wv, Cv).reshape(-1, H, DV)
        attn = jnp.einsum('ehd,ehd->eh', q[edge_src], k)
        amax = jax.ops.segment_max(attn, edge_src, num_segments=n)
        ex = jnp.exp(attn - amax[edge_src])
        denom = jax.ops.segment_sum(ex, edge_src, num_segments=n)
        alpha = ex / (denom[edge_src] + 1e-16)
        upd = jax.ops.segment_sum(v * alpha[..., None], edge_src, num_segments=n)
        upd = upd.reshape(n, OV) @ W_out
        out = tfn_features @ W_self + upd
        mu = out.mean(axis=0)
        var = out.var(axis=0)
        return (out - mu) * jax.lax.rsqrt(var + EPS_BN) * gamma + beta

    def _L1_gnn_ref(v, edge_index, e, W0, b0, W1, b1, W2, b2):
        import jax, jax.numpy as jnp
        import numpy as np
        N_NODES = 6250
        N_EDGES = 100000
        H_DIM = 64

        def scatter_mean(e, receiver, num_segments):
            sums = jax.ops.segment_sum(e, receiver, num_segments=num_segments)
            counts = jax.ops.segment_sum(jnp.ones((e.shape[0],), e.dtype), receiver, num_segments=num_segments)
            return sums / jnp.maximum(counts, 1.0)[:, None]
        receiver = edge_index[1]
        agg = scatter_mean(e, receiver, v.shape[0])
        x = jnp.concatenate([agg, v], axis=-1)
        x = jax.nn.relu(x @ W0 + b0)
        x = jax.nn.relu(x @ W1 + b1)
        x = x @ W2 + b2
        return x
    edge_index = jnp.stack([src, dst])
    x = _layernorm(x + _L0_gnn_ref(x, edge_attr_64, edge_attr_9, L0_gnn_Wq, L0_gnn_Cqk, L0_gnn_Cv, L0_gnn_k_w1, L0_gnn_k_b1, L0_gnn_k_w2, L0_gnn_k_b2, L0_gnn_v_w1, L0_gnn_v_b1, L0_gnn_v_w2, L0_gnn_v_b2, L0_gnn_W_out, L0_gnn_W_self, L0_gnn_gamma, L0_gnn_beta, edge_index), axis=-1)
    x = _layernorm(x + _L1_gnn_ref(x, edge_index, edge_attr_64, L1_gnn_W0, L1_gnn_b0, L1_gnn_W1, L1_gnn_b1, L1_gnn_W2, L1_gnn_b2), axis=-1)
    return x

_drawn_inputs = setup_inputs


def setup_inputs(seed=0):
    import zlib

    import numpy as np

    out = dict(_drawn_inputs(seed))
    spreads = {'L0_gnn_k_b1': (0.0, 0.1),
     'L0_gnn_k_b2': (0.0, 0.1),
     'L0_gnn_v_b1': (0.0, 0.1),
     'L0_gnn_v_b2': (0.0, 0.1),
     'L0_gnn_gamma': (1.0, 0.2),
     'L0_gnn_beta': (0.0, 0.1),
     'L1_gnn_b0': (0.0, 0.1),
     'L1_gnn_b1': (0.0, 0.1),
     'L1_gnn_b2': (0.0, 0.1)}
    factors = {}
    for name, (base, spread) in spreads.items():
        noise = np.random.default_rng([zlib.crc32(name.encode()), seed]).standard_normal(out[name].shape)
        drawn = base * np.exp(spread * noise) if base else spread * noise
        out[name] = jnp.asarray(drawn.astype(out[name].dtype))
    for name, factor in factors.items():
        out[name] = (out[name] * factor).astype(out[name].dtype)
    return out
```

```python
from contextlib import ExitStack

import concourse.bass as bass
from concourse import mybir

fp32 = mybir.dt.float32
f32r = mybir.dt.float32r
bf16 = mybir.dt.bfloat16
i32 = mybir.dt.int32
ALU = mybir.AluOpType
ACT = mybir.ActivationFunctionType
AX = mybir.AxisListType

P = 128
N, E, D, S, H, DH = 12500, 200000, 64, 9, 8, 16
O = H * DH
CH = 512
TC = CH // P
UN = 4
NC = -(-E // (CH * UN)) * UN
EP = NC * CH
EC = EP // P
NT = 100
NP = NT * P
NB = NT // TC
G = 5
ROWS_OK = N // NT
SR = 448
ST = (S + 1) // 2
RW = O + D + H
BIG = 1e30
EPS = 1e-5
assert SR * SR == EP and ROWS_OK * NT == N and NT % TC == 0


class Chunk:

    def __init__(self, i, r):
        self.i, self.r = i, r

    def __add__(self, k):
        return Chunk(self.i, self.r + k)

    def value(self):
        return self.i * UN + self.r

    def slot(self, n):
        return self.r % n

    def turn(self, n):
        return self.i * (UN // n) + self.r // n


def past(i):
    return not isinstance(i, int) or i > 0


def turns_of(engine, n, turn):
    turn(0)
    with engine.Fori(1, n) as i:
        turn(i)


def gnn_kernel(nc, xg, xT, idx, dnow, dbefore, shT, eT, Wq, Ctp, W1, b1, Wk2, Wv2, b2, Wout, Wself, gamma, beta,
               M0, mb0, M1, mb1, M2, mb2, bsel, hsel, ident, mean64, out):
    dram = lambda name, shape, dt: nc.dram_tensor(name, shape, dt, kind="Internal").ap()
    qtab = dram("qtab", (NP, O), fp32)
    newd = dram("newd", (EP,), bf16)
    shp = dram("shp", (3, S * EP), bf16)
    rows = dram("rows", (EP, RW), fp32)

    ctx = ExitStack()
    with ctx:
        def sb(name, shape, dt=fp32):
            return ctx.enter_context(nc.sbuf_tensor(name, shape, dt))

        def pb(name, shape, dt=fp32):
            return ctx.enter_context(nc.psum_tensor(name, shape, dt))

        def sem(name):
            return ctx.enter_context(nc.semaphore(name))

        wq = sb("wq", [D, O])
        chi = sb("chi", [P, ST, 2 * O], f32r)
        clo = sb("clo", [P, ST, 2 * O], f32r)
        w1 = sb("w1", [D, P])
        b1c = sb("b1c", [P, 1])
        w2 = sb("w2", [P, 2, O])
        b2c = sb("b2c", [P, 2])
        wout = sb("wout", [O, P])
        wself = sb("wself", [D, P])
        gb = sb("gb", [D, 2])
        m0a = sb("m0a", [D, P])
        m0b = sb("m0b", [D, P])
        m1 = sb("m1", [D, P])
        m2 = sb("m2", [D, P])
        mb = sb("mb", [D, 3])
        bs = sb("bs", [3 * S, ST, P], bf16)
        hs = sb("hs", [P, P])
        idn = sb("idn", [P, P])
        mn = sb("mn", [D, P])
        epsc = sb("epsc", [P, 1])
        endn = sb("endn", [P, NT + 1])
        lasti = sb("lasti", [P, NT], i32)
        some = sb("some", [P, NT])
        inv = sb("inv", [P, NT])

        banks = [pb(f"bank{i}", [P, 512]) for i in range(8)]

        load = sem("load")
        pool_passed, sp_passed = sem("pool_passed"), sem("sp_passed")
        with ExitStack() as prep:
            ps = lambda name, shape, dt=fp32: prep.enter_context(nc.sbuf_tensor(name, shape, dt))
            ctp = ps("ctp", [P, ST, 2 * O])
            xq = ps("xq", [D, G, CH])
            dcur = ps("dcur", [P, EC], i32)
            dprv = ps("dprv", [P, EC], i32)
            same = ps("same", [P, EC])
            neg = ps("neg", [P, EC], bf16)
            lastd = ps("lastd", [P, SR], i32)
            nodei = ps("nodei", [P, NT + 1], i32)
            nodef = ps("nodef", [P, NT + 1])
            rowf = ps("rowf", [P, NT + 1])
            rowi = ps("rowi", [P, NT + 1], i32)
            rslot = ps("rslot", [P, 2], i32)
            grow = ps("grow", [P, 2, SR], i32)
            cmpo = ps("cmpo", [P, SR])
            cmpo2 = ps("cmpo2", [P, 2, SR])
            inrow = ps("inrow", [P, NT + 1])
            tmpc = ps("tmpc", [P, NT + 1])
            shin = ps("shin", [P, 2, EC])
            shr = ps("shr", [P, EC])
            shm = ps("shm", [P, EC])
            shb = ps("shb", [P, 2, 3, EC], bf16)
            qs = ps("qs", [P, G, TC, O])

            loads2 = sem("loads2")
            shl = [sem(f"sh_loaded{i}") for i in range(2)]
            shs = [sem(f"sh_stored{i}") for i in range(2)]
            shd = sem("sh_split")
            negd, negs = sem("newd_made"), sem("newd_stored")
            qd, qe = sem("q_made"), sem("q_copied")
            qst = [sem(f"q_stored{i}") for i in range(G)]
            xq_in = [sem(f"x_in{i}") for i in range(G)]
            level1 = sem("level1")
            nodes_made, rows_counted, nodef_made = sem("nodes_made"), sem("rows_counted"), sem("nodef_made")
            rslot_made = sem("rslot_made")
            got = [sem(f"search_row{i}") for i in range(2)]
            counted, dve_done = [sem(f"counted{i}") for i in range(2)], sem("prep_dve")

            with nc.Block() as block:
                @block.sync
                def _(sp):
                    sp.dma_start(wq[:, :], Wq).then_inc(loads2, 16)
                    sp.dma_start(dcur[:, :], dnow.rearrange("(p c) -> p c", p=P)).then_inc(loads2, 16)
                    sp.dma_start(dprv[:, :], dbefore.rearrange("(p c) -> p c", p=P)).then_inc(loads2, 16)
                    with nc.allow_non_contiguous_dma(reason="one destination of each search row"):
                        last = dnow.rearrange("(r c) -> r c", c=SR)[:, SR - 1:SR].rearrange("r c -> (r c)")
                        sp.dma_start(lastd[:, :], last.partition_broadcast(P)).then_inc(loads2, 16)
                    for dst, src in ((ctp[:, :, :], Ctp), (w1[:, :], W1), (b1c[:, :], b1), (b2c[:, :], b2),
                                     (wout[:, :], Wout), (wself[:, :], Wself), (gb[:, 0:1], gamma), (gb[:, 1:2], beta),
                                     (m0a[:, :], M0[0:D, :]), (m0b[:, :], M0[D:2 * D, :]), (m1[:, :], M1),
                                     (m2[:, :], M2), (mb[:, 0:1], mb0), (mb[:, 1:2], mb1), (mb[:, 2:3], mb2),
                                     (bs[:, :, :], bsel), (hs[:, :], hsel), (idn[:, :], ident), (mn[:, :], mean64)):
                        sp.dma_start(dst, src).then_inc(load, 16)
                    sp.wait_ge(dve_done, 1)
                    sp.dma_start(w2[0:D, 0, :], Wk2).then_inc(load, 16)
                    sp.dma_start(w2[D:P, 1, :], Wv2).then_inc(load, 16)
                    sp.wait_ge(negd, 2)
                    sp.dma_start(newd.rearrange("(p c) -> p c", p=P), neg[:, :]).then_inc(negs, 16)
                    for s in range(S + 1):
                        if s < S:
                            if s >= 2:
                                sp.wait_ge(shd, 4 * (s - 1))
                            sp.dma_start(shin[:, s % 2, :], shT[s].rearrange("(p c) -> p c", p=P)).then_inc(shl[s % 2], 16)
                        if s >= 1:
                            k = s - 1
                            sp.wait_ge(shd, 4 * (k + 1))
                            dst = shp[:, k * EP:(k + 1) * EP].rearrange("j (p c) -> p j c", p=P)
                            sp.dma_start(dst, shb[:, k % 2, :, :]).then_inc(shs[k % 2], 16)
                    view = qtab.rearrange("(p t) o -> p t o", t=NT)
                    def turn(i):
                        for j in range(G):
                            if past(i):
                                sp.wait_ge(qd, i * G)
                            sp.dma_start(xq[:, j, :], xT[:, bass.ds(i * G * CH + j * CH, CH)]).then_inc(xq_in[j], 16)
                        for j in range(G):
                            sp.wait_ge(qe, i * G + (j + 1))
                            sp.dma_start(view[:, bass.ds(i * G * TC + j * TC, TC), :], qs[:, j, :, :]).then_inc(qst[j], 16)

                    turns_of(sp, NB // G, turn)
                    sp.wait_ge(load, 16 * 21)
                    sp.wait_ge(negs, 16)
                    sp.wait_ge(shs[0], 16 * 5)
                    sp.wait_ge(shs[1], 16 * 4)
                    for j in range(G):
                        sp.wait_ge(qst[j], 16 * (NB // G))

                @block.tensor
                def _(pe):
                    pe.wait_ge(loads2, 16 * 4)
                    def turn(i):
                        for j in range(G):
                            pe.wait_ge(xq_in[j], i * 16 + 16)
                            if past(i):
                                pe.wait_ge(qe, i * G)
                            for k in range(TC):
                                mm = nc.tensor.matmul(banks[j][:, k * O:(k + 1) * O], xq[:, j, k * P:(k + 1) * P],
                                                      wq[:, :], start=True, stop=True)
                            mm.then_inc(qd, 1)

                    turns_of(pe, NB // G, turn)

                @block.scalar
                def _(act):
                    def turn(i):
                        for j in range(G):
                            act.wait_ge(qd, i * G + (j + 1))
                            if past(i):
                                act.wait_ge(qst[j], i * 16)
                            nc.scalar.activation(qs[:, j, :, :], banks[j][:, :].rearrange("p (t o) -> p t o", t=TC),
                                                 ACT.Copy).then_inc(qe, 1)

                    turns_of(act, NB // G, turn)

                @block.gpsimd
                def _(pool):
                    nc.gpsimd.iota(nodei[:, :], pattern=[[1, NT + 1]], base=-1,
                                   channel_multiplier=NT).then_inc(nodes_made, 1)
                    pool.wait_ge(rows_counted, 1)
                    dview = dnow.rearrange("(r c) -> r c", c=SR)

                    def search_row(j, turn, s):
                        if past(turn):
                            pool.wait_ge(counted[s], turn)
                        pool.sem_inc(pool_passed, 1)
                        nc.gpsimd.tensor_copy(rslot[:, s:s + 1], rowi[:, bass.ds(j, 1)]).then_inc(rslot_made, 1)
                        pool.wait_ge(rslot_made, j + 1)
                        pool.sem_inc(pool_passed, 1)
                        nc.gpsimd.indirect_dma_start(
                            out=grow[:, s, :], out_offset=None, in_=dview,
                            in_offset=bass.IndirectOffsetOnAxis(ap=rslot[:, s:s + 1], axis=0),
                        ).then_inc(got[s], 16)

                    def turn(i):
                        for s in range(2):
                            search_row(i * 2 + s, i, s)

                    turns_of(pool, NT // 2, turn)
                    search_row(NT, NT // 2, 0)

                @block.vector
                def _(dve):
                    v = nc.vector
                    step = sem("prep_step")
                    n = [0]

                    def done(ins):
                        ins.then_inc(step, 1)
                        n[0] += 1
                        dve.wait_ge(step, n[0])

                    v.memset(w2[:, :, :], 0.0).then_inc(dve_done, 1)
                    v.memset(epsc[:, :], EPS).then_inc(dve_done, 1)
                    dve.wait_ge(loads2, 16 * 4)
                    dve.wait_ge(load, 16 * 21)
                    done(v.tensor_copy(chi[:, :, :], ctp[:, :, :]))
                    done(v.tensor_tensor(clo[:, :, :], ctp[:, :, :], chi[:, :, :].bitcast(fp32), ALU.subtract))
                    dve.wait_ge(nodes_made, 1)
                    done(v.tensor_copy(nodef[:, :], nodei[:, :]))
                    def turn(j):
                        if past(j):
                            dve.wait_ge(level1, j)
                        v.tensor_scalar(cmpo[:, :], lastd[:, :], nodef[:, bass.ds(j, 1)], 0.0, ALU.is_le, ALU.add,
                                        accum_out=rowf[:, bass.ds(j, 1)]).then_inc(level1, 1)

                    turns_of(dve, NT + 1, turn)
                    dve.wait_ge(level1, NT + 1)
                    v.tensor_copy(rowi[:, :], rowf[:, :]).then_inc(rows_counted, 1)
                    v.tensor_tensor(same[:, :], dcur[:, :], dprv[:, :], ALU.is_equal).then_inc(negd, 1)
                    dve.wait_ge(negd, 1)
                    v.tensor_scalar(neg[:, :], same[:, :], 1.0, BIG, ALU.subtract, ALU.mult).then_inc(negd, 1)
                    for s in range(S):
                        dve.wait_ge(shl[s % 2], 16 * (s // 2 + 1))
                        if s >= 2:
                            dve.wait_ge(shs[s % 2], 16 * (s // 2))
                        k = s % 2
                        c = 4 * s
                        v.tensor_copy(shb[:, k, 0, :], shin[:, k, :]).then_inc(shd, 1)
                        dve.wait_ge(shd, c + 1)
                        v.tensor_tensor(shr[:, :], shin[:, k, :], shb[:, k, 0, :], ALU.subtract).then_inc(shd, 1)
                        dve.wait_ge(shd, c + 2)
                        v.tensor_copy(shb[:, k, 1, :], shr[:, :]).then_inc(shd, 1)
                        dve.wait_ge(shd, c + 3)
                        v.tensor_tensor(shb[:, k, 2, :], shr[:, :], shb[:, k, 1, :], ALU.subtract).then_inc(shd, 1)
                        dve.wait_ge(shd, c + 4)
                    def count_row(j, turn, s):
                        dve.wait_ge(got[s], turn * 16 + 16)
                        v.tensor_scalar(cmpo2[:, s, :], grow[:, s, :], nodef[:, bass.ds(j, 1)], 0.0, ALU.is_le, ALU.add,
                                        accum_out=inrow[:, bass.ds(j, 1)]).then_inc(counted[s], 1)

                    def turn(i):
                        for s in range(2):
                            if past(i):
                                dve.wait_ge(counted[s], i)
                            count_row(i * 2 + s, i, s)

                    turns_of(dve, NT // 2, turn)
                    dve.wait_ge(counted[0], NT // 2)
                    count_row(NT, NT // 2, 0)
                    dve.wait_ge(counted[0], NT // 2 + 1)
                    dve.wait_ge(counted[1], NT // 2)
                    done(v.tensor_scalar(tmpc[:, :], rowf[:, :], float(SR), None, ALU.mult))
                    done(v.tensor_tensor(endn[:, :], tmpc[:, :], inrow[:, :], ALU.add))
                    done(v.tensor_scalar(tmpc[:, 0:NT], endn[:, 1:NT + 1], -1.0, 0.0, ALU.add, ALU.max))
                    done(v.tensor_copy(lasti[:, :], tmpc[:, 0:NT]))
                    done(v.tensor_tensor(inv[:, :], endn[:, 1:NT + 1], endn[:, 0:NT], ALU.subtract))
                    done(v.tensor_scalar(some[:, :], inv[:, :], 1.0, None, ALU.min))
                    done(v.tensor_scalar(tmpc[:, 0:NT], inv[:, :], 1.0, None, ALU.max))
                    done(v.reciprocal(inv[:, :], tmpc[:, 0:NT]))
                    done(v.tensor_tensor(inv[:, :], inv[:, :], some[:, :], ALU.mult))

        with ExitStack() as main:
            ms = lambda name, shape, dt=fp32: main.enter_context(nc.sbuf_tensor(name, shape, dt))
            idx_all = ms("idx_all", [P, 2 * EC], i32)
            idxs = ms("idxs", [P, 2, 2 * TC], i32)
            gx = ms("gx", [P, 2, TC, 2 * D])
            gq = ms("gq", [P, 2, TC, O])
            v2 = ms("v2", [D + H, UN, CH])
            hp = ms("hp", [3 * S, UN, CH], bf16)
            nm = ms("nm", [P, UN, CH], bf16)
            xd = ms("xd", [P, 2, CH])
            hid = ms("hid", [P, 2, CH])
            wk = ms("wk", [P, 2, CH])
            wv = ms("wv", [P, 2, CH])
            z = ms("z", [P, ST, CH])
            zhi = ms("zhi", [P, 2, ST, CH], f32r)
            zlo = ms("zlo", [P, 2, ST - 1, CH], f32r)
            wkq = ms("wkq", [P, 2, CH])
            kq = ms("kq", [P, 2, CH])
            vv = ms("vv", [P, 2, CH])
            mx = ms("mx", [P, 2, CH + 1])
            mprev = ms("mprev", [P, 2, CH])
            argd = ms("argd", [P, 2, CH])
            argp = ms("argp", [P, 2, CH])
            prob = ms("prob", [P, 2, CH])
            dec = ms("dec", [P, 2, CH])
            d2 = ms("d2", [D + H, 2, CH])
            pv = ms("pv", [P, 2, CH])
            n1 = ms("n1", [P, 2, CH])
            n2 = ms("n2", [D + H, 2, CH])
            ot = ms("ot", [P, 2, TC, RW])

            pair = banks[0:2]
            sbank = banks[2:4]
            tpk, tpv, qbank, abank = banks[4:8]

            e_in = [sem(f"edges_in{i}") for i in range(UN)]
            h_in = [sem(f"harmonics_in{i}") for i in range(UN)]
            n_in = [sem(f"newd_in{i}") for i in range(UN)]
            x_in = [sem(f"x_gathered{i}") for i in range(2)]
            q_in = [sem(f"q_gathered{i}") for i in range(2)]
            o_out = [sem(f"rows_stored{i}") for i in range(2)]
            idx_in, idx_made = sem("idx_in"), sem("idx_made")
            pair_full, pair_free = sem("pair_full"), sem("pair_copied")
            shb_full, z_done, zhi_done, zlo_done = sem("shb_full"), sem("z_done"), sem("zhi_done"), sem("zlo_done")
            tpk_full, tpv_full, q_full, a_full = sem("tpk_full"), sem("tpv_full"), sem("q_full"), sem("attn_full")
            wkq_done, kq_done, v_done = sem("wkq_done"), sem("kq_done"), sem("v_done")
            m_done, mcol_done, argp_done = sem("max_done"), sem("maxcol_done"), sem("argp_done")
            mprev_done, argd_done = sem("mprev_done"), sem("argd_done")
            prob_done, prob2_done, dec_done, mask_done, dec2_done = (
                sem("prob_done"), sem("prob2_done"), sem("dec_done"), sem("mask_done"), sem("dec2_done"))
            pv_done, n1_done, n2_done = sem("pv_done"), sem("n1_done"), sem("n2_done")
            zeroed = sem("zeroed")

            X_, HID, WK, WV, ROWA, ROWB = range(6)

            def use(t, k):
                if isinstance(t.i, int):
                    n = t.value()
                    if n <= 0:
                        return 4 * (n + 1) + k
                    if n >= NC - 1:
                        return 6 * (NC - 1) + 2 + 2 * (n - NC + 1) + k - 4
                    return 6 * n + 2 + k
                return t.value() * 6 + 2 + k

            def front_use(c, k):
                return use(c + (-1), k)

            def steps(engine, step):
                def has(n):
                    return n + 1 < NC, 0 <= n < NC, 1 <= n <= NC

                first, turns = 3, (NC - 6) // UN
                for n in range(-1, first):
                    step(Chunk(0, n), *has(n))
                with engine.Fori(0, turns) as i:
                    for k in range(UN):
                        step(Chunk(i, first + k), True, True, True)
                for n in range(first + UN * turns, NC + 1):
                    step(Chunk(0, n), *has(n))

            with nc.Block() as block:
                @block.sync
                def _(sp):
                    sp.dma_start(idx_all[:, :], idx).then_inc(idx_in, 16)
                    sp.wait_ge(zeroed, 3)

                    def loads(c):
                        s, t = c.slot(UN), c.turn(UN)
                        at = c.value() * CH
                        old = c + (-UN)
                        first = isinstance(c.i, int) and c.value() < UN
                        if not first:
                            sp.wait_ge(n2_done, old.value() + 1)
                            sp.sem_inc(sp_passed, 1)
                            sp.wait_ge(shb_full, (old.value() + 1) * ST)
                            sp.sem_inc(sp_passed, 1)
                            sp.wait_ge(mprev_done, old.value() + 1)
                            sp.sem_inc(sp_passed, 1)
                            sp.wait_ge(mask_done, old.value() + 1)
                            sp.sem_inc(sp_passed, 1)
                        sp.dma_start(v2[0:D, s, :], eT[:, bass.ds(at, CH)]).then_inc(e_in[s], 16)
                        part = shp.rearrange("j (s e) -> (j s) e", s=S)
                        sp.dma_start(hp[:, s, :], part[:, bass.ds(at, CH)]).then_inc(h_in[s], 16)
                        sp.dma_start(nm[:, s, :], newd[bass.ds(at, CH)].partition_broadcast(P)).then_inc(n_in[s], 16)

                    def store(c):
                        s = c.slot(2)
                        row = use(c + 1, ROWB)
                        sp.wait_ge(pair_free, row + 1)
                        dst = rows[bass.ds(c.value() * CH, CH), :].rearrange("(t p) w -> p t w", p=P)
                        sp.dma_start(dst, ot[:, s, :, :]).then_inc(o_out[s], 16)

                    for n in range(2):
                        loads(Chunk(0, n))

                    def step(t, front, mid, rear):
                        if not (isinstance(t.i, int) and t.value() + 3 >= NC):
                            loads(t + 3)
                        if rear:
                            store(t + (-1))

                    steps(sp, step)
                    for s in range(2):
                        sp.wait_ge(o_out[s], 16 * (NC // 2))

                @block.gpsimd
                def _(pool):
                    def gathers(c):
                        s = c.slot(2)
                        first = isinstance(c.i, int) and c.value() < 2
                        if not first:
                            pool.wait_ge(pair_full, front_use(c + (-2), X_) + 1)
                            pool.wait_ge(q_full, c.value() - 1)
                        pool.sem_inc(pool_passed, 1)
                        nc.gpsimd.tensor_copy(idxs[:, s, :], idx_all[:, bass.ds(c.value() * 2 * TC, 2 * TC)])\
                            .then_inc(idx_made, 1)
                        pool.wait_ge(idx_made, c.value() + 1)
                        pool.sem_inc(pool_passed, 1)
                        for k in range(TC):
                            nc.gpsimd.indirect_dma_start(
                                out=gx[:, s, k, :], out_offset=None, in_=xg[:, :],
                                in_offset=bass.IndirectOffsetOnAxis(ap=idxs[:, s, k:k + 1], axis=0),
                            ).then_inc(x_in[s], 16)
                        for k in range(TC):
                            nc.gpsimd.indirect_dma_start(
                                out=gq[:, s, k, :], out_offset=None, in_=qtab[:, :],
                                in_offset=bass.IndirectOffsetOnAxis(ap=idxs[:, s, TC + k:TC + k + 1], axis=0),
                            ).then_inc(q_in[s], 16)

                    def softmax_args(c):
                        s = c.slot(2)
                        n = c.value() + 1
                        pool.wait_ge(m_done, n)
                        pool.wait_ge(n_in[c.slot(UN)], 16 * (c.turn(UN) + 1))
                        if not (isinstance(c.i, int) and c.value() < 2):
                            pool.wait_ge(dec_done, n - 2)
                        nc.gpsimd.tensor_tensor(mprev[:, s, :], mx[:, s, 0:CH], nm[:, c.slot(UN), :],
                                                ALU.add).then_inc(mprev_done, 1)
                        pool.wait_ge(mprev_done, n)
                        nc.gpsimd.tensor_tensor(argd[:, s, :], mprev[:, s, :], mx[:, s, 1:CH + 1],
                                                ALU.subtract).then_inc(argd_done, 1)

                    pool.wait_ge(idx_in, 16)
                    gathers(Chunk(0, 0))

                    def step(t, front, mid, rear):
                        if rear:
                            softmax_args(t + (-1))
                        if not (isinstance(t.i, int) and t.value() + 2 >= NC):
                            gathers(t + 2)

                    steps(pool, step)

                @block.scalar
                def _(act):
                    def take(t, k):
                        n = use(t, k)
                        act.wait_ge(pair_full, n + 1)
                        return pair[k % 2]

                    def old(c, by):
                        return not (isinstance(c.i, int) and c.value() < by)

                    def step(t, front, mid, rear):
                        c = t + 1
                        if front:
                            s = c.slot(2)
                            bank = take(t, X_)
                            if old(c, 2):
                                act.wait_ge(z_done, (c.value() - 1) * ST)
                            nc.scalar.activation(xd[:, s, :], bank[:, :], ACT.Copy).then_inc(pair_free, 1)
                            bank = take(t, HID)
                            nc.scalar.activation(hid[:, s, :], bank[:, :], ACT.Relu, bias=b1c[:, 0:1]).then_inc(pair_free, 1)
                        if rear:
                            b = t + (-1)
                            s, n = b.slot(2), b.value() + 1
                            act.wait_ge(argp_done, n)
                            if old(b, 2):
                                act.wait_ge(pv_done, n - 2)
                            nc.scalar.activation(prob[:, s, :], argp[:, s, :], ACT.Exp).then_inc(prob_done, 1)
                            nc.scalar.activation(v2[D:D + H, b.slot(UN), :], argp[D:D + H, s, :], ACT.Exp)\
                                .then_inc(prob2_done, 1)
                            act.wait_ge(n_in[b.slot(UN)], 16 * (b.turn(UN) + 1))
                            if old(b, 2):
                                act.wait_ge(n2_done, n - 2)
                            nc.scalar.activation(d2[0:D, s, :], nm[0:D, b.slot(UN), :], ACT.Relu, bias=1.0)\
                                .then_inc(mask_done, 1)
                            act.wait_ge(argd_done, n)
                            if old(b, 2):
                                act.wait_ge(n1_done, n - 2)
                            nc.scalar.activation(dec[:, s, :], argd[:, s, :], ACT.Exp).then_inc(dec_done, 1)
                            nc.scalar.activation(d2[D:D + H, s, :], argd[D:D + H, s, :], ACT.Exp).then_inc(dec2_done, 1)
                        if front:
                            s = c.slot(2)
                            if old(c, 2):
                                act.wait_ge(tpv_full, c.value() - 1)
                            for a, b in ((0, 3), (3, ST)):
                                act.wait_ge(z_done, c.value() * ST + b)
                                nc.scalar.activation(zhi[:, s, a:b, :], z[:, a:b, :], ACT.Copy).then_inc(zhi_done, 1)
                            bank = take(t, WK)
                            if old(c, 2):
                                act.wait_ge(wkq_done, c.value() - 1)
                            nc.scalar.activation(wk[:, s, :], bank[:, :], ACT.Identity, bias=b2c[:, 0:1]).then_inc(pair_free, 1)
                            bank = take(t, WV)
                            if old(c, 2):
                                act.wait_ge(v_done, c.value() - 1)
                            nc.scalar.activation(wv[:, s, :], bank[:, :], ACT.Identity, bias=b2c[:, 1:2]).then_inc(pair_free, 1)
                        if rear:
                            b = t + (-1)
                            s = b.slot(2)
                            if old(b, 2):
                                act.wait_ge(o_out[s], 16 * b.turn(2))
                            for half, k in enumerate((ROWA, ROWB)):
                                bank = take(t, k)
                                nc.scalar.activation(ot[:, s, 2 * half:2 * half + 2, :],
                                                     bank[:, :].rearrange("p (t w) -> p t w", t=2)[:, :, 0:RW],
                                                     ACT.Copy).then_inc(pair_free, 1)

                    steps(act, step)

                @block.vector
                def _(dve):
                    v = nc.vector
                    v.memset(mx[:, 0, 0:1], 0.0).then_inc(zeroed, 1)
                    v.memset(n1[:, 1, CH - 1:CH], 0.0).then_inc(zeroed, 1)
                    v.memset(n2[:, 1, CH - 1:CH], 0.0).then_inc(zeroed, 1)
                    dve.wait_ge(zeroed, 3)

                    def old(c, by):
                        return not (isinstance(c.i, int) and c.value() < by)

                    def step(t, front, mid, rear):
                        if mid:
                            s, n = t.slot(2), t.value() + 1
                            dve.wait_ge(wkq_done, n)
                            dve.wait_ge(tpk_full, n)
                            v.tensor_tensor(kq[:, s, :], tpk[:, :], wkq[:, s, :], ALU.mult).then_inc(kq_done, 1)
                        if front:
                            c = t + 1
                            s = c.slot(2)
                            dve.wait_ge(pair_free, front_use(c, X_) + 1)
                            for j in range(ST):
                                dve.wait_ge(shb_full, c.value() * ST + j + 1)
                                if j == 0 and old(c, 1):
                                    dve.wait_ge(zlo_done, c.value() * 2)
                                v.tensor_tensor(z[:, j, :], sbank[(s + j) % 2][:, :], xd[:, s, :],
                                                ALU.mult).then_inc(z_done, 1)
                        if rear:
                            b = t + (-1)
                            s, n = b.slot(2), b.value() + 1
                            dve.wait_ge(prob_done, n)
                            dve.wait_ge(v_done, n)
                            v.tensor_tensor(pv[:, s, :], vv[:, s, :], prob[:, s, :], ALU.mult).then_inc(pv_done, 1)
                            dve.wait_ge(pv_done, n)
                            dve.wait_ge(dec_done, n)
                            if old(b, 1):
                                dve.wait_ge(n2_done, n - 1)
                            if old(b, 2):
                                dve.wait_ge(pair_full, use(t + (-2), ROWB) + 1)
                            v.tensor_tensor_scan(n1[:, s, :], dec[:, s, :], pv[:, s, :], n1[:, 1 - s, CH - 1:CH],
                                                 ALU.mult, ALU.add).then_inc(n1_done, 1)
                            dve.wait_ge(prob2_done, n)
                            dve.wait_ge(mask_done, n)
                            dve.wait_ge(dec2_done, n)
                            v.tensor_tensor_scan(n2[:, s, :], d2[:, s, :], v2[:, b.slot(UN), :],
                                                 n2[:, 1 - s, CH - 1:CH], ALU.mult, ALU.add).then_inc(n2_done, 1)
                        if front:
                            c = t + 1
                            s, n = c.slot(2), c.value() + 1
                            dve.wait_ge(zhi_done, 2 * n)
                            if old(c, 2):
                                dve.wait_ge(tpv_full, n - 2)
                            v.tensor_tensor(zlo[:, s, :, :], z[:, 0:ST - 1, :], zhi[:, s, 0:ST - 1, :].bitcast(fp32),
                                            ALU.subtract).then_inc(zlo_done, 1)
                            v.tensor_tensor(zhi[D:P, s, ST - 1, :], z[D:P, ST - 1, :],
                                            zhi[D:P, s, ST - 1, :].bitcast(fp32), ALU.subtract).then_inc(zlo_done, 1)
                            dve.wait_ge(q_full, n)
                            dve.wait_ge(pair_free, front_use(c, WK) + 1)
                            if old(c, 2):
                                dve.wait_ge(kq_done, n - 2)
                            v.tensor_tensor(wkq[:, s, :], qbank[:, :], wk[:, s, :], ALU.mult).then_inc(wkq_done, 1)
                        if mid:
                            s, n = t.slot(2), t.value() + 1
                            dve.wait_ge(tpv_full, n)
                            dve.wait_ge(pair_free, front_use(t, WV) + 1)
                            v.tensor_tensor(vv[:, s, :], tpv[:, :], wv[:, s, :], ALU.mult).then_inc(v_done, 1)
                            dve.wait_ge(a_full, n)
                            dve.wait_ge(n_in[t.slot(UN)], 16 * (t.turn(UN) + 1))
                            if old(t, 1):
                                dve.wait_ge(mcol_done, n - 1)
                                dve.wait_ge(argd_done, n - 1)
                            v.tensor_tensor_scan(mx[:, s, 1:CH + 1], nm[:, t.slot(UN), :], abank[:, :], mx[:, s, 0:1],
                                                 ALU.add, ALU.max).then_inc(m_done, 1)
                            dve.wait_ge(m_done, n)
                            if old(t, 2):
                                dve.wait_ge(prob2_done, n - 2)
                            v.tensor_tensor(argp[:, s, :], abank[:, :], mx[:, s, 1:CH + 1], ALU.subtract).then_inc(argp_done, 1)
                            v.tensor_copy(mx[:, 1 - s, 0:1], mx[:, s, CH:CH + 1]).then_inc(mcol_done, 1)

                    steps(dve, step)

                @block.tensor
                def _(pe):
                    def take(t, k):
                        n = use(t, k)
                        if not (isinstance(t.i, int) and n < 2):
                            pe.wait_ge(pair_free, n - 1)
                        return pair[k % 2]

                    def old(c, by):
                        return not (isinstance(c.i, int) and c.value() < by)

                    def step(t, front, mid, rear):
                        c = t + 1
                        cs = c.slot(2)

                        def spread(j):
                            n = c.value() * ST + j
                            if not (isinstance(c.i, int) and n < 2):
                                pe.wait_ge(z_done, n - 1)
                            nc.tensor.matmul(sbank[(cs + j) % 2][:, :], bs[:, j, :], hp[:, c.slot(UN), :],
                                             start=True, stop=True).then_inc(shb_full, 1)

                        def product(out, o, s, j):
                            hi, lo = chi[:, j, o:o + O], clo[:, j, o:o + O]
                            nc.tensor.matmul(out[:, :], hi, zhi[:, s, j, :], start=(j == 0), stop=False)
                            if j < ST - 1:
                                nc.tensor.matmul(out[:, :], hi, zlo[:, s, j, :], start=False, stop=False)
                                return nc.tensor.matmul(out[:, :], lo, zhi[:, s, j, :], start=False, stop=False)
                            return nc.tensor.matmul(out[:, :], lo[0:D, :], zhi[0:D, s, j, :], start=False, stop=True)

                        if front:
                            bank = take(t, X_)
                            pe.wait_ge(x_in[cs], 16 * TC * (c.turn(2) + 1))
                            for k in range(TC):
                                mm = nc.tensor.transpose(bank[:, k * P:(k + 1) * P], gx[:, cs, k, :], idn[:, :])
                            mm.then_inc(pair_full, 1)
                            bank = take(t, HID)
                            pe.wait_ge(e_in[c.slot(UN)], 16 * (c.turn(UN) + 1))
                            nc.tensor.matmul(bank[:, :], w1[:, :], v2[0:D, c.slot(UN), :],
                                             start=True, stop=True).then_inc(pair_full, 1)
                        if mid:
                            s, n = t.slot(2), t.value() + 1
                            pe.wait_ge(zlo_done, n * 2)
                            if old(t, 1):
                                pe.wait_ge(kq_done, n - 1)
                            for j in range(ST):
                                mm = product(tpk, 0, s, j)
                            mm.then_inc(tpk_full, 1)
                        if front:
                            pe.wait_ge(h_in[c.slot(UN)], 16 * (c.turn(UN) + 1))
                            spread(0)
                            spread(1)
                            bank = take(t, WK)
                            pe.wait_ge(pair_free, use(t, HID) + 1)
                            nc.tensor.matmul(bank[:, :], w2[:, 0, :], hid[:, cs, :], start=True, stop=True)\
                                .then_inc(pair_full, 1)
                        if mid:
                            if old(t, 1):
                                pe.wait_ge(v_done, n - 1)
                            for j in range(ST):
                                mm = product(tpv, O, s, j)
                                if front and 1 <= j <= 3:
                                    spread(j + 1)
                            mm.then_inc(tpv_full, 1)
                        elif front:
                            for j in range(2, ST):
                                spread(j)
                        if front:
                            bank = take(t, WV)
                            nc.tensor.matmul(bank[:, :], w2[:, 1, :], hid[:, cs, :], start=True, stop=True)\
                                .then_inc(pair_full, 1)
                            pe.wait_ge(q_in[cs], 16 * TC * (c.turn(2) + 1))
                            if old(c, 1):
                                pe.wait_ge(wkq_done, c.value())
                            for k in range(TC):
                                mm = nc.tensor.transpose(qbank[:, k * P:(k + 1) * P], gq[:, cs, k, :], idn[:, :])
                            mm.then_inc(q_full, 1)
                        if mid:
                            pe.wait_ge(kq_done, n)
                            if old(t, 1):
                                pe.wait_ge(argp_done, n - 1)
                            nc.tensor.matmul(abank[:, :], hs[:, :], kq[:, s, :], start=True, stop=True)\
                                .then_inc(a_full, 1)
                        if rear:
                            b = t + (-1)
                            s, n = b.slot(2), b.value() + 1
                            pe.wait_ge(n2_done, n)
                            for half, k in enumerate((ROWA, ROWB)):
                                bank = take(t, k)
                                for m in range(2):
                                    e0 = (2 * half + m) * P
                                    nc.tensor.transpose(bank[:, 256 * m:256 * m + O], n1[:, s, e0:e0 + P], idn[:, :])
                                    mm = nc.tensor.transpose(bank[:, 256 * m + O:256 * m + RW], n2[:, s, e0:e0 + P],
                                                             idn[0:D + H, 0:D + H])
                                mm.then_inc(pair_full, 1)

                    steps(pe, step)

        with ExitStack() as fin:
            fs = lambda name, shape, dt=fp32: fin.enter_context(nc.sbuf_tensor(name, shape, dt))
            o0 = fs("o0", [D, NP])
            ag = fs("ag", [D, NP])
            lslot = fs("lslot", [P, G, TC], i32)
            xs = fs("xs", [D, G, CH])
            st = fs("st", [D, 8])
            parts = fs("parts", [D, 10])

            each = lambda name: [sem(f"{name}{i}") for i in range(G)]
            x_l, g_l, x2_l, y_s = each("x_loaded"), each("rows_gathered"), each("x_again"), each("y_stored")
            av_zero = sem("av_zero")
            lslot_made, den_ok, rec_made, rec_some, up_made, av_made = (
                sem("lslot_made"), sem("den_ok"), sem("rec_made"), sem("rec_some"), sem("up_made"), sem("av_made"))
            upT_made, upT_copied, avT_made, avT_copied, o0_made, o0_copied = (
                sem("upT_made"), sem("upT_copied"), sem("avT_made"), sem("avT_copied"), sem("o0_made"), sem("o0_copied"))
            st_d, st_a = sem("stats_dve"), sem("stats_act")
            SS = {k: sem(f"{k}_made") for k in ("r", "y", "mean", "dd", "sq", "var", "sd", "rs", "x1", "z0", "h0", "z1",
                                                "h1", "z2", "y2", "mean2", "dd2", "sq2", "var2", "sd2", "rs2", "o")}

            def at(i, j):
                return bass.ds(i * G * CH + j * CH, CH)

            with ExitStack() as fin1:
                f1 = lambda name, shape, dt=fp32: fin1.enter_context(nc.sbuf_tensor(name, shape, dt))
                gr = f1("gr", [P, G, TC, RW])
                rec = f1("rec", [P, G, 3, TC * H])
                up = f1("up", [P, G, TC, O])
                av = f1("av", [P, G, TC, P])
                upT = f1("upT", [P, G, CH])

                with nc.Block() as block:
                    @block.sync
                    def _(sp):
                        def turn(i):
                            for j in range(G):
                                if past(i):
                                    sp.wait_ge(o0_made, i * G)
                                sp.dma_start(xs[:, j, :], xT[:, at(i, j)]).then_inc(x_l[j], 16)

                        turns_of(sp, NB // G, turn)

                    @block.gpsimd
                    def _(pool):
                        def turn(i):
                            for j in range(G):
                                if past(i):
                                    pool.wait_ge(av_made, i * G)
                                pool.sem_inc(pool_passed, 1)
                                nc.gpsimd.tensor_copy(lslot[:, j, :], lasti[:, bass.ds(i * G * TC + j * TC, TC)])\
                                    .then_inc(lslot_made, 1)
                                pool.wait_ge(lslot_made, i * G + (j + 1))
                                pool.sem_inc(pool_passed, 1)
                                for k in range(TC):
                                    nc.gpsimd.indirect_dma_start(
                                        out=gr[:, j, k, :], out_offset=None, in_=rows[:, :],
                                        in_offset=bass.IndirectOffsetOnAxis(ap=lslot[:, j, k:k + 1], axis=0),
                                    ).then_inc(g_l[j], 16)

                        turns_of(pool, NB // G, turn)

                    @block.tensor
                    def _(pe):
                        t = nc.tensor
                        def turn(i):
                            for j in range(G):
                                pe.wait_ge(up_made, i * G + (j + 1))
                                if past(i):
                                    pe.wait_ge(o0_copied, i * G)
                                for k in range(TC):
                                    mm = t.transpose(banks[j][:, k * P:(k + 1) * P], up[:, j, k, :], idn[:, :])
                                mm.then_inc(upT_made, 1)
                            for j in range(G):
                                pe.wait_ge(upT_copied, i * G + (j + 1))
                                pe.wait_ge(av_made, i * G + (j + 1))
                                for k in range(TC):
                                    mm = t.transpose(banks[j][:, k * P:(k + 1) * P], av[:, j, k, :], idn[:, :])
                                mm.then_inc(avT_made, 1)
                            for j in range(G):
                                pe.wait_ge(avT_copied, i * G + (j + 1))
                                pe.wait_ge(x_l[j], i * 16 + 16)
                                t.matmul(banks[j][:, :], wself[:, :], xs[:, j, :], start=True, stop=False)
                                t.matmul(banks[j][:, :], wout[:, :], upT[:, j, :], start=False, stop=True).then_inc(o0_made, 1)

                        turns_of(pe, NB // G, turn)

                    @block.scalar
                    def _(act):
                        f = nc.scalar.activation
                        def turn(i):
                            for j in range(G):
                                act.wait_ge(upT_made, i * G + (j + 1))
                                if past(i):
                                    act.wait_ge(o0_made, i * G)
                                f(upT[:, j, :], banks[j][:, :], ACT.Copy).then_inc(upT_copied, 1)
                            for j in range(G):
                                act.wait_ge(avT_made, i * G + (j + 1))
                                f(ag[:, at(i, j)], banks[j][0:D, :], ACT.Copy).then_inc(avT_copied, 1)
                            for j in range(G):
                                act.wait_ge(o0_made, i * G + (j + 1))
                                f(o0[:, at(i, j)], banks[j][0:D, :], ACT.Copy).then_inc(o0_copied, 1)

                        turns_of(act, NB // G, turn)

                    @block.vector
                    def _(dve):
                        v = nc.vector
                        v.memset(av[:, :, :, :], 0.0).then_inc(av_zero, 1)
                        dve.wait_ge(av_zero, 1)

                        def turn(i):
                            for j in range(G):
                                n = i * G + (j + 1)
                                tl = bass.ds(i * G * TC + j * TC, TC)
                                dve.wait_ge(g_l[j], i * 16 * TC + 16 * TC)
                                rv = [rec[:, j, q, :].rearrange("p (t h) -> p t h", h=H) for q in range(3)]
                                if past(i):
                                    dve.wait_ge(up_made, i * G)
                                v.tensor_scalar(rv[0], gr[:, j, :, O + D:RW], 1e-16, None, ALU.add).then_inc(den_ok, 1)
                                dve.wait_ge(den_ok, n)
                                v.reciprocal(rv[1], rv[0]).then_inc(rec_made, 1)
                                dve.wait_ge(rec_made, n)
                                v.tensor_tensor(rv[2], rv[1], some[:, tl].unsqueeze(2).broadcast_to([P, TC, H]),
                                                ALU.mult).then_inc(rec_some, 1)
                                dve.wait_ge(rec_some, n)
                                if past(i):
                                    dve.wait_ge(upT_made, i * G)
                                if past(i):
                                    dve.wait_ge(avT_made, i * G)
                                v.tensor_tensor(up[:, j, :, :].rearrange("p t (d h) -> p t d h", h=H),
                                                gr[:, j, :, 0:O].rearrange("p t (d h) -> p t d h", h=H),
                                                rv[2].unsqueeze(2).broadcast_to([P, TC, DH, H]), ALU.mult).then_inc(up_made, 1)
                                v.tensor_tensor(av[:, j, :, 0:D], gr[:, j, :, O:O + D],
                                                inv[:, tl].unsqueeze(2).broadcast_to([P, TC, D]), ALU.mult).then_inc(av_made, 1)

                        turns_of(dve, NB // G, turn)

            with ExitStack() as fin2:
                f2 = lambda name, shape, dt=fp32: fin2.enter_context(nc.sbuf_tensor(name, shape, dt))
                junk = f2("junk", [D, NT * ROWS_OK // 10], bf16)
                work = {k: f2(f"{k}_", [D, G, CH]) for k in ("r", "y", "dd", "sq", "sd", "rs", "x1")}
                work |= {"h0": work["r"], "y2": work["r"], "h1": work["y"]}

                with nc.Block() as block:
                    @block.sync
                    def _(sp):
                        def turn(i):
                            for j in range(G):
                                if past(i):
                                    sp.wait_ge(SS["r"], i * G)
                                sp.dma_start(xs[:, j, :], xT[:, at(i, j)]).then_inc(x2_l[j], 16)
                            for j in range(G):
                                sp.wait_ge(SS["o"], i * G + (j + 1))
                                sp.dma_start(out[:, at(i, j)], work["sq"][:, j, :]).then_inc(y_s[j], 16)

                        turns_of(sp, NB // G, turn)
                        for j in range(G):
                            sp.wait_ge(y_s[j], 16 * (NB // G))

                    @block.tensor
                    def _(pe):
                        t = nc.tensor

                        def mm64(name, lhsT, after, src, i):
                            for j in range(G):
                                pe.wait_ge(SS[after], i * G + (j + 1))
                                t.matmul(banks[j][:, :], lhsT[:, :], work[src][:, j, :], start=True, stop=True)\
                                    .then_inc(SS[name], 1)

                        def turn(i):
                            mm64("mean", mn, "y", "y", i)
                            mm64("var", mn, "sq", "sq", i)
                            for j in range(G):
                                pe.wait_ge(SS["x1"], i * G + (j + 1))
                                t.matmul(banks[j][:, :], m0a[:, :], ag[:, at(i, j)], start=True, stop=False)
                                t.matmul(banks[j][:, :], m0b[:, :], work["x1"][:, j, :], start=False, stop=True)\
                                    .then_inc(SS["z0"], 1)
                            mm64("z1", m1, "h0", "h0", i)
                            mm64("z2", m2, "h1", "h1", i)
                            mm64("mean2", mn, "y2", "y2", i)
                            mm64("var2", mn, "sq2", "sq", i)

                        turns_of(pe, NB // G, turn)

                    @block.scalar
                    def _(act):
                        f = nc.scalar.activation
                        act.wait_ge(st_d, 2)
                        ov = o0[:, :].rearrange("d (t p) -> d t p", p=P)
                        for q in range(10):
                            if q:
                                act.wait_ge(st_a, q)
                            f(junk[:, :].rearrange("d (t p) -> d t p", p=ROWS_OK),
                              ov[:, q * NT // 10:(q + 1) * NT // 10, 0:ROWS_OK], ACT.Square, bias=st[:, 1:2],
                              accum_out=parts[:, q:q + 1]).then_inc(st_a, 1)
                        act.wait_ge(st_d, 3)
                        f(st[:, 3:4], st[:, 2:3], ACT.Sqrt, bias=epsc[0:D, 0:1], scale=1.0 / N).then_inc(st_a, 1)

                        def each_block(name, after, fn, i):
                            for j in range(G):
                                act.wait_ge(SS[after], i * G + (j + 1))
                                fn(j).then_inc(SS[name], 1)

                        act.wait_ge(st_d, 7)
                        def turn(i):
                            for j in range(G):
                                act.wait_ge(x2_l[j], i * 16 + 16)
                                if past(i):
                                    act.wait_ge(SS["o"], i * G)
                                f(work["r"][:, j, :], xs[:, j, :], ACT.Identity, bias=st[:, 6:7]).then_inc(SS["r"], 1)
                            for j in range(G):
                                if past(i):
                                    act.wait_ge(y_s[j], i * 16)
                                act.wait_ge(SS["dd"], i * G + (j + 1))
                                f(work["sq"][:, j, :], work["dd"][:, j, :], ACT.Square).then_inc(SS["sq"], 1)
                            each_block("sd", "var", lambda j: f(work["sd"][:, j, :], banks[j][0:D, :], ACT.Sqrt,
                                                                bias=epsc[0:D, 0:1]), i)
                            each_block("h0", "z0", lambda j: f(work["h0"][:, j, :], banks[j][0:D, :], ACT.Relu,
                                                               bias=mb[:, 0:1]), i)
                            each_block("h1", "z1", lambda j: f(work["h1"][:, j, :], banks[j][0:D, :], ACT.Relu,
                                                               bias=mb[:, 1:2]), i)
                            each_block("sq2", "dd2", lambda j: f(work["sq"][:, j, :], work["dd"][:, j, :], ACT.Square), i)
                            each_block("sd2", "var2", lambda j: f(work["sd"][:, j, :], banks[j][0:D, :], ACT.Sqrt,
                                                                  bias=epsc[0:D, 0:1]), i)

                        turns_of(act, NB // G, turn)

                    @block.vector
                    def _(dve):
                        v = nc.vector
                        dve.wait_ge(o0_copied, NB)
                        ov = o0[:, :].rearrange("d (t p) -> d t p", p=P)[:, :, 0:ROWS_OK]
                        v.tensor_reduce(st[:, 0:1], ov, AX.XY, ALU.add).then_inc(st_d, 1)
                        dve.wait_ge(st_d, 1)
                        v.tensor_scalar(st[:, 1:2], st[:, 0:1], -1.0 / N, None, ALU.mult).then_inc(st_d, 1)
                        dve.wait_ge(st_a, 10)
                        v.tensor_reduce(st[:, 2:3], parts[:, :], AX.X, ALU.add).then_inc(st_d, 1)
                        dve.wait_ge(st_a, 11)
                        v.reciprocal(st[:, 4:5], st[:, 3:4]).then_inc(st_d, 1)
                        dve.wait_ge(st_d, 4)
                        v.tensor_tensor(st[:, 5:6], st[:, 4:5], gb[:, 0:1], ALU.mult).then_inc(st_d, 1)
                        dve.wait_ge(st_d, 5)
                        v.tensor_tensor(st[:, 7:8], st[:, 5:6], st[:, 1:2], ALU.mult).then_inc(st_d, 1)
                        dve.wait_ge(st_d, 6)
                        v.tensor_tensor(st[:, 6:7], st[:, 7:8], gb[:, 1:2], ALU.add).then_inc(st_d, 1)
                        dve.wait_ge(st_d, 7)

                        def each_block(name, after, fn, i):
                            for j in range(G):
                                dve.wait_ge(SS[after], i * G + (j + 1))
                                fn(j).then_inc(SS[name], 1)

                        W = lambda k, j: work[k][:, j, :]
                        def turn(i):
                            for j in range(G):
                                if past(i):
                                    dve.wait_ge(SS["o"], i * G)
                                dve.wait_ge(SS["r"], i * G + (j + 1))
                                v.scalar_tensor_tensor(out=W("y", j), in0=o0[:, at(i, j)], scalar=st[:, 5:6], in1=W("r", j),
                                                       op0=ALU.mult, op1=ALU.add).then_inc(SS["y"], 1)
                            each_block("dd", "mean", lambda j: v.tensor_tensor(W("dd", j), W("y", j), banks[j][0:D, :],
                                                                               ALU.subtract), i)
                            each_block("rs", "sd", lambda j: v.reciprocal(W("rs", j), W("sd", j)), i)
                            each_block("x1", "rs", lambda j: v.tensor_tensor(W("x1", j), W("dd", j), W("rs", j), ALU.mult), i)
                            each_block("y2", "z2", lambda j: v.scalar_tensor_tensor(
                                out=W("y2", j), in0=banks[j][0:D, :], scalar=mb[:, 2:3], in1=W("x1", j),
                                op0=ALU.add, op1=ALU.add), i)
                            each_block("dd2", "mean2", lambda j: v.tensor_tensor(W("dd", j), W("y2", j), banks[j][0:D, :],
                                                                                 ALU.subtract), i)
                            each_block("rs2", "sd2", lambda j: v.reciprocal(W("rs", j), W("sd", j)), i)
                            each_block("o", "rs2", lambda j: v.tensor_tensor(W("sq", j), W("dd", j), W("rs", j), ALU.mult), i)

                        turns_of(dve, NB // G, turn)



def kernel(**inputs):
    import numpy as np
    import concourse.bacc as bacc
    import ml_dtypes
    from concourse.bass_utils import run_bass_kernel_spmd

    g = {k: np.asarray(v) for k, v in inputs.items()}
    hd = lambda w: np.ascontiguousarray(w.reshape(w.shape[:-1] + (H, DH)).swapaxes(-1, -2).reshape(w.shape))
    pad_e = lambda v, fill: np.concatenate([v, np.full(EP - E, fill, v.dtype)])
    tiles = lambda v: pad_e(v, 0).reshape(NC, TC, P).transpose(2, 0, 1)
    col = lambda v: v.reshape(-1, 1)
    wide = lambda w: np.concatenate([w, np.zeros((w.shape[0], P - w.shape[1]), w.dtype)], axis=1)

    x = g["x"]
    xT = np.zeros((D, NT, P), x.dtype)
    xT[:, :, :ROWS_OK] = x.reshape(ROWS_OK, NT, D).transpose(2, 1, 0)
    both = np.concatenate([hd(g["L0_gnn_Cqk"]), hd(g["L0_gnn_Cv"])], axis=-1)
    ctp = np.zeros((2, D, ST, 2 * O), both.dtype)
    for s in range(S):
        ctp[s % 2, :, s // 2] = both[:, s]
    ctp[1, :, ST - 1] = both[:, S - 1]
    shT = np.zeros((S, EP), np.float32)
    shT[:, :E] = g["edge_attr_9"].T
    eT = np.zeros((D, EP), np.float32)
    eT[:, :E] = g["edge_attr_64"].T

    bsel = np.zeros((3, S, ST, P), np.float32)
    for s in range(S):
        bsel[:, s, s // 2, (s % 2) * D:(s % 2 + 1) * D] = 1
    bsel[:, S - 1, ST - 1, :] = 1
    hsel = (np.arange(P)[:, None] % H == np.arange(P)[None, :] % H).astype(np.float32)

    arrays = {
        "xg": np.concatenate([x, x], axis=1), "xT": xT.reshape(D, NP),
        "idx": np.concatenate([tiles(g["src"]), tiles(g["dst"])], axis=2).reshape(P, NC * 2 * TC),
        "dnow": pad_e(g["dst"], NP), "dbefore": np.concatenate([np.full(1, -1, np.int32), pad_e(g["dst"], NP)[:-1]]),
        "shT": shT, "eT": eT, "Wq": hd(g["L0_gnn_Wq"]), "Ctp": ctp.reshape(P, ST, 2 * O),
        "W1": np.concatenate([g["L0_gnn_k_w1"], g["L0_gnn_v_w1"]], axis=1),
        "b1": col(np.concatenate([g["L0_gnn_k_b1"], g["L0_gnn_v_b1"]])),
        "Wk2": hd(g["L0_gnn_k_w2"]), "Wv2": hd(g["L0_gnn_v_w2"]),
        "b2": np.stack([hd(g["L0_gnn_k_b2"]), hd(g["L0_gnn_v_b2"])], axis=1),
        "Wout": wide(g["L0_gnn_W_out"].reshape(H, DH, D).transpose(1, 0, 2).reshape(O, D)), "Wself": wide(g["L0_gnn_W_self"]),
        "gamma": col(g["L0_gnn_gamma"]), "beta": col(g["L0_gnn_beta"]),
        "M0": wide(g["L1_gnn_W0"]), "mb0": col(g["L1_gnn_b0"]), "M1": wide(g["L1_gnn_W1"]), "mb1": col(g["L1_gnn_b1"]),
        "M2": wide(g["L1_gnn_W2"]), "mb2": col(g["L1_gnn_b2"]),
        "bsel": bsel.reshape(3 * S, ST, P).astype(ml_dtypes.bfloat16), "hsel": hsel,
        "ident": np.eye(P, dtype=np.float32), "mean64": wide(np.full((D, D), 1.0 / D, np.float32)),
    }
    arrays = {f"in_{k}": np.ascontiguousarray(v) for k, v in arrays.items()}
    nc = bacc.Bacc("TRN2", target_bir_lowering=False, num_devices=1)
    args = [nc.dram_tensor(k, v.shape, mybir.dt.from_np(v.dtype), kind="ExternalInput").ap() for k, v in arrays.items()]
    res = nc.dram_tensor("out_y", (D, NP), fp32, kind="ExternalOutput").ap()
    gnn_kernel(nc, *args, res)
    r = run_bass_kernel_spmd(nc, [arrays], core_ids=[0])
    y = r.results[0]["out_y"].reshape(D, NT, P)[:, :, :ROWS_OK]
    return np.ascontiguousarray(y.transpose(2, 1, 0).reshape(N, D))
```

```python
from contextlib import ExitStack

import concourse.bass as bass
from concourse import mybir

fp32 = mybir.dt.float32
f32r = mybir.dt.float32r
bf16 = mybir.dt.bfloat16
i32 = mybir.dt.int32
ALU = mybir.AluOpType
ACT = mybir.ActivationFunctionType
AX = mybir.AxisListType

P = 128
N, E, D, S, H, DH = 12500, 200000, 64, 9, 8, 16
O = H * DH
CH = 512
TC = CH // P
UN = 4
NC = -(-E // (CH * UN)) * UN
EP = NC * CH
EC = EP // P
NT = 100
NP = NT * P
NB = NT // TC
G = 5
HC = NP // 2
NN, GN = 16, 8
CN = HC // NN
ROWS_OK = N // NT
SR = 448
ST = (S + 1) // 2
RW = O + D + H
BIG = 1e30
EPS = 1e-5
TURNS = (NC - 6) // UN
assert TURNS <= NT + 1 <= TURNS + NC + 1 - 3 - UN * TURNS
assert SR * SR == EP and ROWS_OK * NT == N and NT % TC == 0


class Chunk:

    def __init__(self, i, r):
        self.i, self.r = i, r

    def __add__(self, k):
        return Chunk(self.i, self.r + k)

    def value(self):
        return self.i * UN + self.r

    def slot(self, n):
        return self.r % n

    def turn(self, n):
        return self.i * (UN // n) + self.r // n


def past(i):
    return not isinstance(i, int) or i > 0


def turns_of(engine, n, turn):
    turn(0)
    with engine.Fori(1, n) as i:
        turn(i)


def gnn_kernel(nc, xg, xT, idx, dnow, dbefore, shT, eT, Wq, Ctp, W1, b1, Wk2, Wv2, b2, Wout, Wself, gamma_beta,
               M0e, M0x, M1, M2, mbias, bsel, hsel, ident, mean64, halves, xP, out):
    dram = lambda name, shape, dt: nc.dram_tensor(name, shape, dt, kind="Internal").ap()
    qtab = dram("qtab", (NP, O), fp32)
    newd = dram("newd", (EP,), bf16)
    shp = dram("shp", (3, S * EP), bf16)
    rows = dram("rows", (EP, RW), fp32)

    ctx = ExitStack()
    with ctx:
        def sb(name, shape, dt=fp32):
            return ctx.enter_context(nc.sbuf_tensor(name, shape, dt))

        def pb(name, shape, dt=fp32):
            return ctx.enter_context(nc.psum_tensor(name, shape, dt))

        def sem(name):
            return ctx.enter_context(nc.semaphore(name))

        wq = sb("wq", [D, O])
        chi = sb("chi", [P, ST, 2 * O], f32r)
        clo = sb("clo", [P, ST, 2 * O], f32r)
        w1 = sb("w1", [D, P])
        b1c = sb("b1c", [P, 1])
        w2 = sb("w2", [P, 2, O])
        b2c = sb("b2c", [P, 2])
        wout = sb("wout", [O, 2, P])
        wself = sb("wself", [P, P])
        m0e = sb("m0e", [P, P])
        m0x = sb("m0x", [P, P])
        m1 = sb("m1", [P, P])
        m2 = sb("m2", [P, P])
        mn = sb("mn", [P, P])
        fold = sb("fold", [P, P])
        gb = sb("gb", [P, 2])
        mb = sb("mb", [P, 3])
        bs = sb("bs", [3 * S, ST, P], bf16)
        hs = sb("hs", [P, P])
        idn = sb("idn", [P, P])
        epsc = sb("epsc", [P, 1])
        nodeh = sb("nodeh", [P, NT + 1])
        rowc = sb("rowc", [P, NT + 1])
        inrow = sb("inrow", [P, NT + 1])

        banks = [pb(f"bank{i}", [P, 512]) for i in range(8)]

        load = sem("load")
        pool_passed, sp_passed, act_passed = sem("pool_passed"), sem("sp_passed"), sem("act_passed")
        with ExitStack() as prep:
            ps = lambda name, shape, dt=fp32: prep.enter_context(nc.sbuf_tensor(name, shape, dt))
            ctp = ps("ctp", [P, ST, 2 * O])
            xq = ps("xq", [D, G, CH])
            qs = ps("qs", [P, G, TC, O])
            dcur = ps("dcur", [P, EC], i32)
            dprv = ps("dprv", [P, EC], i32)
            same = ps("same", [P, EC])
            neg = ps("neg", [P, EC], bf16)
            nodei = ps("nodei", [P, NT + 1], i32)
            shin = ps("shin", [P, 3, EC])
            shr = ps("shr", [P, 2, EC])
            parts3 = ps("parts3", [P, 3, 3, EC], bf16)

            dst_in, w2_zero, nodes_made = sem("dst_in"), sem("w2_zero"), sem("nodes_made")
            w_split, neg_made, neg_stored = sem("w_split"), sem("neg_made"), sem("neg_stored")
            sh_in = [sem(f"sh_in{i}") for i in range(3)]
            sh_out = [sem(f"sh_out{i}") for i in range(3)]
            first_made, rest_made, second_made, third_made = (
                sem("first_made"), sem("rest_made"), sem("second_made"), sem("third_made"))
            q_made, q_copied = sem("q_made"), sem("q_copied")
            xq_in = [sem(f"xq_in{i}") for i in range(G)]
            q_out = [sem(f"q_out{i}") for i in range(G)]
            wq_in = sem("wq_in")

            with nc.Block() as block:
                @block.sync
                def _(sp):
                    def harmonic_in(s):
                        if s >= 3:
                            sp.wait_ge(third_made, s - 2)
                        sp.dma_start(shin[:, s % 3, :], shT[s].rearrange("(p c) -> p c", p=P)).then_inc(sh_in[s % 3], 16)

                    sp.dma_start(wq[:, :], Wq).then_inc(wq_in, 16)
                    harmonic_in(0)
                    harmonic_in(1)
                    sp.dma_start(dcur[:, :], dnow.rearrange("(p c) -> p c", p=P)).then_inc(dst_in, 16)
                    sp.dma_start(dprv[:, :], dbefore.rearrange("(p c) -> p c", p=P)).then_inc(dst_in, 16)
                    harmonic_in(2)
                    sp.dma_start(ctp[:, :, :], Ctp).then_inc(dst_in, 16)
                    consts = ((w1[:, :], W1), (b1c[:, :], b1), (b2c[:, :], b2), (wout[:, :, :], Wout),
                              (wself[:, :], Wself), (gb[:, :], gamma_beta), (m0e[:, :], M0e), (m0x[:, :], M0x),
                              (m1[:, :], M1), (m2[:, :], M2), (mb[:, :], mbias), (bs[:, :, :], bsel), (hs[:, :], hsel),
                              (idn[:, :], ident), (mn[:, :], mean64), (fold[:, :], halves))
                    for dst, src in consts:
                        sp.dma_start(dst, src).then_inc(load, 16)
                    sp.wait_ge(w2_zero, 1)
                    sp.dma_start(w2[0:D, 0, :], Wk2).then_inc(load, 16)
                    sp.dma_start(w2[D:P, 1, :], Wv2).then_inc(load, 16)
                    for s in range(S):
                        sp.wait_ge(third_made, s + 1)
                        dst = shp[:, s * EP:(s + 1) * EP].rearrange("j (p c) -> p j c", p=P)
                        sp.dma_start(dst, parts3[:, s % 3, :, :]).then_inc(sh_out[s % 3], 16)
                        if s + 3 < S:
                            harmonic_in(s + 3)
                    sp.wait_ge(neg_made, 2)
                    sp.dma_start(newd.rearrange("(p c) -> p c", p=P), neg[:, :]).then_inc(neg_stored, 16)
                    sp.wait_ge(load, 16 * (len(consts) + 2))
                    sp.wait_ge(neg_stored, 16)
                    for k in range(3):
                        sp.wait_ge(sh_out[k], 16 * (S // 3))

                @block.tensor
                def _(pe):
                    pe.wait_ge(wq_in, 16)

                    def turn(i):
                        for j in range(G):
                            pe.wait_ge(xq_in[j], i * 16 + 16)
                            if past(i):
                                pe.wait_ge(q_copied, (i - 1) * G + (j + 1))
                            for k in range(TC):
                                mm = nc.tensor.matmul(banks[j][:, k * O:(k + 1) * O], xq[:, j, k * P:(k + 1) * P],
                                                      wq[:, :], start=True, stop=True)
                            mm.then_inc(q_made, 1)

                    turns_of(pe, NB // G, turn)

                @block.scalar
                def _(act):
                    view = qtab.rearrange("(p t) o -> p t o", t=NT)

                    def x_in_block(i, j):
                        act.dma_start(xq[:, j, :], xT[:, bass.ds(i * G * CH + j * CH, CH)]).then_inc(xq_in[j], 16)

                    def turn(i, more=True):
                        for j in range(G):
                            n = i * G + (j + 1)
                            act.wait_ge(q_made, n)
                            if more:
                                x_in_block(i + 1, j)
                            if past(i):
                                act.wait_ge(q_out[j], i * 16)
                            nc.scalar.activation(qs[:, j, :, :], banks[j][:, :].rearrange("p (t o) -> p t o", t=TC),
                                                 ACT.Copy).then_inc(q_copied, 1)
                            act.wait_ge(q_copied, n)
                            act.dma_start(view[:, bass.ds(i * G * TC + j * TC, TC), :], qs[:, j, :, :]).then_inc(q_out[j], 16)

                    for j in range(G):
                        x_in_block(0, j)
                    last = NB // G - 1
                    turns_of(act, last, turn)
                    turn(last, more=False)
                    for j in range(G):
                        act.wait_ge(q_out[j], 16 * (NB // G))

                @block.gpsimd
                def _(pool):
                    nc.gpsimd.iota(nodei[:, :], pattern=[[1, NT + 1]], base=-1,
                                   channel_multiplier=NT).then_inc(nodes_made, 1)
                    for s in range(S + 1):
                        if s < S:
                            pool.wait_ge(sh_in[s % 3], 16 * (s // 3 + 1))
                            if s >= 3:
                                pool.wait_ge(sh_out[s % 3], 16 * (s // 3))
                            nc.gpsimd.tensor_copy(parts3[:, s % 3, 0, :], shin[:, s % 3, :]).then_inc(first_made, 1)
                        if s >= 1:
                            k = s - 1
                            pool.wait_ge(rest_made, k + 1)
                            nc.gpsimd.tensor_copy(parts3[:, k % 3, 1, :], shr[:, k % 2, :]).then_inc(second_made, 1)

                @block.vector
                def _(dve):
                    v = nc.vector
                    v.memset(w2[:, :, :], 0.0).then_inc(w2_zero, 1)
                    v.memset(epsc[:, :], EPS)
                    dve.wait_ge(nodes_made, 1)
                    v.tensor_scalar(nodeh[:, :], nodei[:, :], 0.5, None, ALU.add)
                    for s in range(S + 1):
                        if s < S:
                            dve.wait_ge(first_made, s + 1)
                            if s >= 2:
                                dve.wait_ge(third_made, s - 1)
                            v.tensor_tensor(shr[:, s % 2, :], shin[:, s % 3, :], parts3[:, s % 3, 0, :],
                                            ALU.subtract).then_inc(rest_made, 1)
                        if s == 0:
                            dve.wait_ge(dst_in, 16 * 3)
                            v.tensor_copy(chi[:, :, :], ctp[:, :, :]).then_inc(w_split, 1)
                            dve.wait_ge(w_split, 1)
                            v.tensor_tensor(clo[:, :, :], ctp[:, :, :], chi[:, :, :].bitcast(fp32), ALU.subtract)
                        if s == 1:
                            v.tensor_tensor(same[:, :], dcur[:, :], dprv[:, :], ALU.is_equal).then_inc(neg_made, 1)
                            dve.wait_ge(neg_made, 1)
                            v.tensor_scalar(neg[:, :], same[:, :], 1.0, BIG, ALU.subtract, ALU.mult).then_inc(neg_made, 1)
                        if s >= 1:
                            k = s - 1
                            dve.wait_ge(second_made, k + 1)
                            v.tensor_tensor(parts3[:, k % 3, 2, :], shr[:, k % 2, :], parts3[:, k % 3, 1, :],
                                            ALU.subtract).then_inc(third_made, 1)

        with ExitStack() as main:
            ms = lambda name, shape, dt=fp32: main.enter_context(nc.sbuf_tensor(name, shape, dt))
            idx_all = ms("idx_all", [P, 2 * EC], i32)
            idxs = ms("idxs", [P, 2, 2 * TC], i32)
            gx = ms("gx", [P, 2, TC, 2 * D])
            gq = ms("gq", [P, 2, TC, O])
            v2 = ms("v2", [D + H, UN, CH])
            hp = ms("hp", [3 * S, UN, CH], bf16)
            nm = ms("nm", [P, UN, CH], bf16)
            xd = ms("xd", [P, 2, CH])
            hid = ms("hid", [P, 2, CH])
            wk = ms("wk", [P, 2, CH])
            wv = ms("wv", [P, 2, CH])
            z = ms("z", [P, ST, CH])
            zhi = ms("zhi", [P, 2, ST, CH], f32r)
            zlo = ms("zlo", [P, 2, ST - 1, CH], f32r)
            wkq = ms("wkq", [P, 2, CH])
            kq = ms("kq", [P, 2, CH])
            vv = ms("vv", [P, 2, CH])
            mx = ms("mx", [P, 2, CH + 1])
            mprev = ms("mprev", [P, 2, CH])
            argd = ms("argd", [P, 2, CH])
            argp = ms("argp", [P, 2, CH])
            prob = ms("prob", [P, 2, CH])
            dec = ms("dec", [P, 2, CH])
            d2 = ms("d2", [D + H, 2, CH])
            pv = ms("pv", [P, 2, CH])
            n1 = ms("n1", [P, 2, CH])
            n2 = ms("n2", [D + H, 2, CH])
            ot = ms("ot", [P, 2, TC, RW])
            lastd = ms("lastd", [P, SR], i32)
            grow = ms("grow", [P, SR], i32)
            rslot = ms("rslot", [P, 1], i32)
            signs = ms("signs", [P, SR], bf16)

            pair = banks[0:2]
            sbank = banks[2:4]
            tpk, tpv, qbank, abank = banks[4:8]

            e_in = [sem(f"edges_in{i}") for i in range(UN)]
            h_in = [sem(f"harmonics_in{i}") for i in range(UN)]
            n_in = [sem(f"newd_in{i}") for i in range(UN)]
            x_in = [sem(f"x_gathered{i}") for i in range(2)]
            q_in = [sem(f"q_gathered{i}") for i in range(2)]
            o_out = [sem(f"rows_stored{i}") for i in range(2)]
            idx_in, idx_made = sem("idx_in"), sem("idx_made")
            pair_full, pair_free = sem("pair_full"), sem("pair_copied")
            shb_full, z_done, zhi_done, zlo_done = sem("shb_full"), sem("z_done"), sem("zhi_done"), sem("zlo_done")
            tpk_full, tpv_full, q_full, a_full = sem("tpk_full"), sem("tpv_full"), sem("q_full"), sem("attn_full")
            wkq_done, kq_done, v_done = sem("wkq_done"), sem("kq_done"), sem("v_done")
            m_done, mcol_done, argp_done = sem("max_done"), sem("maxcol_done"), sem("argp_done")
            mprev_done, argd_done = sem("mprev_done"), sem("argd_done")
            prob_done, prob2_done, dec_done, mask_done, dec2_done = (
                sem("prob_done"), sem("prob2_done"), sem("dec_done"), sem("mask_done"), sem("dec2_done"))
            pv_done, n1_done, n2_done = sem("pv_done"), sem("n1_done"), sem("n2_done")
            zeroed = sem("zeroed")
            lastd_in, row_found, row_slot, row_in, row_counted = (
                sem("lastd_in"), sem("row_found"), sem("row_slot"), sem("row_in"), sem("row_counted"))

            X_, HID, WK, WV, ROWA, ROWB = range(6)

            def use(t, k):
                if isinstance(t.i, int):
                    n = t.value()
                    if n <= 0:
                        return 4 * (n + 1) + k
                    if n >= NC - 1:
                        return 6 * (NC - 1) + 2 + 2 * (n - NC + 1) + k - 4
                    return 6 * n + 2 + k
                return t.value() * 6 + 2 + k

            def front_use(c, k):
                return use(c + (-1), k)

            def steps(engine, step):
                def has(n):
                    return n + 1 < NC, 0 <= n < NC, 1 <= n <= NC

                for n in range(-1, 3):
                    step(Chunk(0, n), *has(n), None, None)
                with engine.Fori(0, TURNS) as i:
                    for k in range(UN):
                        step(Chunk(i, 3 + k), True, True, True, i if k == 0 else None, i if k == 3 else None)
                for n in range(3 + UN * TURNS, NC + 1):
                    m = n - 3 - (UN - 1) * TURNS
                    step(Chunk(0, n), *has(n), m if m <= NT else None, m - 1 if TURNS <= m - 1 <= NT else None)

            with nc.Block() as block:
                @block.sync
                def _(sp):
                    sp.dma_start(idx_all[:, :], idx).then_inc(idx_in, 16)
                    with nc.allow_non_contiguous_dma(reason="one destination of each search row"):
                        last = dnow.rearrange("(r c) -> r c", c=SR)[:, SR - 1:SR].rearrange("r c -> (r c)")
                        sp.dma_start(lastd[:, :], last.partition_broadcast(P)).then_inc(lastd_in, 16)
                    sp.wait_ge(zeroed, 3)

                    def loads(c):
                        s, t = c.slot(UN), c.turn(UN)
                        at = c.value() * CH
                        old = c + (-UN)
                        first = isinstance(c.i, int) and c.value() < UN
                        if not first:
                            sp.wait_ge(n2_done, old.value() + 1)
                            sp.sem_inc(sp_passed, 1)
                            sp.wait_ge(shb_full, (old.value() + 1) * ST)
                            sp.sem_inc(sp_passed, 1)
                            sp.wait_ge(mprev_done, old.value() + 1)
                            sp.sem_inc(sp_passed, 1)
                            sp.wait_ge(mask_done, old.value() + 1)
                            sp.sem_inc(sp_passed, 1)
                        sp.dma_start(v2[0:D, s, :], eT[:, bass.ds(at, CH)]).then_inc(e_in[s], 16)
                        part = shp.rearrange("j (s e) -> (j s) e", s=S)
                        sp.dma_start(hp[:, s, :], part[:, bass.ds(at, CH)]).then_inc(h_in[s], 16)
                        sp.dma_start(nm[:, s, :], newd[bass.ds(at, CH)].partition_broadcast(P)).then_inc(n_in[s], 16)

                    def store(c):
                        s = c.slot(2)
                        row = use(c + 1, ROWB)
                        sp.wait_ge(pair_free, row + 1)
                        dst = rows[bass.ds(c.value() * CH, CH), :].rearrange("(t p) w -> p t w", p=P)
                        sp.dma_start(dst, ot[:, s, :, :]).then_inc(o_out[s], 16)

                    for n in range(2):
                        loads(Chunk(0, n))

                    def step(t, front, mid, rear, find, count):
                        if not (isinstance(t.i, int) and t.value() + 3 >= NC):
                            loads(t + 3)
                        if rear:
                            store(t + (-1))

                    steps(sp, step)
                    for s in range(2):
                        sp.wait_ge(o_out[s], 16 * (NC // 2))

                @block.gpsimd
                def _(pool):
                    def gathers(c):
                        s = c.slot(2)
                        first = isinstance(c.i, int) and c.value() < 2
                        if not first:
                            pool.wait_ge(pair_full, front_use(c + (-2), X_) + 1)
                            pool.wait_ge(q_full, c.value() - 1)
                        pool.sem_inc(pool_passed, 1)
                        nc.gpsimd.tensor_copy(idxs[:, s, :], idx_all[:, bass.ds(c.value() * 2 * TC, 2 * TC)])\
                            .then_inc(idx_made, 1)
                        pool.wait_ge(idx_made, c.value() + 1)
                        pool.sem_inc(pool_passed, 1)
                        for k in range(TC):
                            nc.gpsimd.indirect_dma_start(
                                out=gx[:, s, k, :], out_offset=None, in_=xg[:, :],
                                in_offset=bass.IndirectOffsetOnAxis(ap=idxs[:, s, k:k + 1], axis=0),
                            ).then_inc(x_in[s], 16)
                        for k in range(TC):
                            nc.gpsimd.indirect_dma_start(
                                out=gq[:, s, k, :], out_offset=None, in_=qtab[:, :],
                                in_offset=bass.IndirectOffsetOnAxis(ap=idxs[:, s, TC + k:TC + k + 1], axis=0),
                            ).then_inc(q_in[s], 16)

                    def softmax_args(c):
                        s = c.slot(2)
                        n = c.value() + 1
                        pool.wait_ge(m_done, n)
                        pool.wait_ge(n_in[c.slot(UN)], 16 * (c.turn(UN) + 1))
                        if not (isinstance(c.i, int) and c.value() < 2):
                            pool.wait_ge(dec_done, n - 2)
                        nc.gpsimd.tensor_tensor(mprev[:, s, :], mx[:, s, 0:CH], nm[:, c.slot(UN), :],
                                                ALU.add).then_inc(mprev_done, 1)
                        pool.wait_ge(mprev_done, n)
                        nc.gpsimd.tensor_tensor(argd[:, s, :], mprev[:, s, :], mx[:, s, 1:CH + 1],
                                                ALU.subtract).then_inc(argd_done, 1)

                    pool.wait_ge(idx_in, 16)
                    gathers(Chunk(0, 0))

                    def step(t, front, mid, rear, find, count):
                        if rear:
                            softmax_args(t + (-1))
                        if not (isinstance(t.i, int) and t.value() + 2 >= NC):
                            gathers(t + 2)
                        if find is not None:
                            pool.wait_ge(row_slot, find + 1)
                            pool.sem_inc(pool_passed, 1)
                            nc.gpsimd.indirect_dma_start(
                                out=grow[:, :], out_offset=None, in_=dnow.rearrange("(r c) -> r c", c=SR),
                                in_offset=bass.IndirectOffsetOnAxis(ap=rslot[:, 0:1], axis=0)).then_inc(row_in, 16)

                    steps(pool, step)

                @block.scalar
                def _(act):
                    def take(t, k):
                        n = use(t, k)
                        act.wait_ge(pair_full, n + 1)
                        return pair[k % 2]

                    def old(c, by):
                        return not (isinstance(c.i, int) and c.value() < by)

                    def step(t, front, mid, rear, find, count):
                        c = t + 1
                        if front:
                            s = c.slot(2)
                            bank = take(t, X_)
                            if old(c, 2):
                                act.wait_ge(z_done, (c.value() - 1) * ST)
                            nc.scalar.activation(xd[:, s, :], bank[:, :], ACT.Copy).then_inc(pair_free, 1)
                            bank = take(t, HID)
                            nc.scalar.activation(hid[:, s, :], bank[:, :], ACT.Relu, bias=b1c[:, 0:1]).then_inc(pair_free, 1)
                        if rear:
                            b = t + (-1)
                            s, n = b.slot(2), b.value() + 1
                            act.wait_ge(argp_done, n)
                            if old(b, 2):
                                act.wait_ge(pv_done, n - 2)
                            nc.scalar.activation(prob[:, s, :], argp[:, s, :], ACT.Exp).then_inc(prob_done, 1)
                            nc.scalar.activation(v2[D:D + H, b.slot(UN), :], argp[D:D + H, s, :], ACT.Exp)\
                                .then_inc(prob2_done, 1)
                            act.wait_ge(n_in[b.slot(UN)], 16 * (b.turn(UN) + 1))
                            if old(b, 2):
                                act.wait_ge(n2_done, n - 2)
                            nc.scalar.activation(d2[0:D, s, :], nm[0:D, b.slot(UN), :], ACT.Relu, bias=1.0)\
                                .then_inc(mask_done, 1)
                            act.wait_ge(argd_done, n)
                            if old(b, 2):
                                act.wait_ge(n1_done, n - 2)
                            nc.scalar.activation(dec[:, s, :], argd[:, s, :], ACT.Exp).then_inc(dec_done, 1)
                            nc.scalar.activation(d2[D:D + H, s, :], argd[D:D + H, s, :], ACT.Exp).then_inc(dec2_done, 1)
                        if front:
                            s = c.slot(2)
                            if old(c, 2):
                                act.wait_ge(tpv_full, c.value() - 1)
                            for a, b in ((0, 3), (3, ST)):
                                act.wait_ge(z_done, c.value() * ST + b)
                                nc.scalar.activation(zhi[:, s, a:b, :], z[:, a:b, :], ACT.Copy).then_inc(zhi_done, 1)
                            bank = take(t, WK)
                            if old(c, 2):
                                act.wait_ge(wkq_done, c.value() - 1)
                            nc.scalar.activation(wk[:, s, :], bank[:, :], ACT.Identity, bias=b2c[:, 0:1]).then_inc(pair_free, 1)
                            bank = take(t, WV)
                            if old(c, 2):
                                act.wait_ge(v_done, c.value() - 1)
                            nc.scalar.activation(wv[:, s, :], bank[:, :], ACT.Identity, bias=b2c[:, 1:2]).then_inc(pair_free, 1)
                        if rear:
                            b = t + (-1)
                            s = b.slot(2)
                            if old(b, 2):
                                act.wait_ge(o_out[s], 16 * b.turn(2))
                            for half, k in enumerate((ROWA, ROWB)):
                                bank = take(t, k)
                                nc.scalar.activation(ot[:, s, 2 * half:2 * half + 2, :],
                                                     bank[:, :].rearrange("p (t w) -> p t w", t=2)[:, :, 0:RW],
                                                     ACT.Copy).then_inc(pair_free, 1)
                        if count is not None:
                            act.wait_ge(row_in, count * 16 + 16)
                            act.sem_inc(act_passed, 1)
                            nc.scalar.activation(signs[:, :], grow[:, :], ACT.Sign, bias=nodeh[:, bass.ds(count, 1)],
                                                 scale=-1.0, accum_out=inrow[:, bass.ds(count, 1)]).then_inc(row_counted, 1)
                            act.wait_ge(row_counted, count + 1)
                        if find is not None:
                            at = bass.ds(find, 1)
                            act.sem_inc(act_passed, 1)
                            nc.scalar.activation(signs[:, :], lastd[:, :], ACT.Sign, bias=nodeh[:, at], scale=-1.0,
                                                 accum_out=rowc[:, at]).then_inc(row_found, 1)
                            act.wait_ge(row_found, find + 1)
                            act.sem_inc(act_passed, 1)
                            nc.scalar.activation(rslot[:, :], rowc[:, at], ACT.Copy, bias=SR / 2, scale=0.5).then_inc(row_slot, 1)

                    act.wait_ge(lastd_in, 16)
                    steps(act, step)

                @block.vector
                def _(dve):
                    v = nc.vector
                    v.memset(mx[:, 0, 0:1], 0.0).then_inc(zeroed, 1)
                    v.memset(n1[:, 1, CH - 1:CH], 0.0).then_inc(zeroed, 1)
                    v.memset(n2[:, 1, CH - 1:CH], 0.0).then_inc(zeroed, 1)
                    dve.wait_ge(zeroed, 3)

                    def old(c, by):
                        return not (isinstance(c.i, int) and c.value() < by)

                    def step(t, front, mid, rear, find, count):
                        if mid:
                            s, n = t.slot(2), t.value() + 1
                            dve.wait_ge(wkq_done, n)
                            dve.wait_ge(tpk_full, n)
                            v.tensor_tensor(kq[:, s, :], tpk[:, :], wkq[:, s, :], ALU.mult).then_inc(kq_done, 1)
                        if front:
                            c = t + 1
                            s = c.slot(2)
                            dve.wait_ge(pair_free, front_use(c, X_) + 1)
                            for j in range(ST):
                                dve.wait_ge(shb_full, c.value() * ST + j + 1)
                                if j == 0 and old(c, 1):
                                    dve.wait_ge(zlo_done, c.value() * 2)
                                v.tensor_tensor(z[:, j, :], sbank[(s + j) % 2][:, :], xd[:, s, :],
                                                ALU.mult).then_inc(z_done, 1)
                        if rear:
                            b = t + (-1)
                            s, n = b.slot(2), b.value() + 1
                            dve.wait_ge(prob_done, n)
                            dve.wait_ge(v_done, n)
                            v.tensor_tensor(pv[:, s, :], vv[:, s, :], prob[:, s, :], ALU.mult).then_inc(pv_done, 1)
                            dve.wait_ge(pv_done, n)
                            dve.wait_ge(dec_done, n)
                            if old(b, 1):
                                dve.wait_ge(n2_done, n - 1)
                            if old(b, 2):
                                dve.wait_ge(pair_full, use(t + (-2), ROWB) + 1)
                            v.tensor_tensor_scan(n1[:, s, :], dec[:, s, :], pv[:, s, :], n1[:, 1 - s, CH - 1:CH],
                                                 ALU.mult, ALU.add).then_inc(n1_done, 1)
                            dve.wait_ge(prob2_done, n)
                            dve.wait_ge(mask_done, n)
                            dve.wait_ge(dec2_done, n)
                            v.tensor_tensor_scan(n2[:, s, :], d2[:, s, :], v2[:, b.slot(UN), :],
                                                 n2[:, 1 - s, CH - 1:CH], ALU.mult, ALU.add).then_inc(n2_done, 1)
                        if front:
                            c = t + 1
                            s, n = c.slot(2), c.value() + 1
                            dve.wait_ge(zhi_done, 2 * n)
                            if old(c, 2):
                                dve.wait_ge(tpv_full, n - 2)
                            v.tensor_tensor(zlo[:, s, :, :], z[:, 0:ST - 1, :], zhi[:, s, 0:ST - 1, :].bitcast(fp32),
                                            ALU.subtract).then_inc(zlo_done, 1)
                            v.tensor_tensor(zhi[D:P, s, ST - 1, :], z[D:P, ST - 1, :],
                                            zhi[D:P, s, ST - 1, :].bitcast(fp32), ALU.subtract).then_inc(zlo_done, 1)
                            dve.wait_ge(q_full, n)
                            dve.wait_ge(pair_free, front_use(c, WK) + 1)
                            if old(c, 2):
                                dve.wait_ge(kq_done, n - 2)
                            v.tensor_tensor(wkq[:, s, :], qbank[:, :], wk[:, s, :], ALU.mult).then_inc(wkq_done, 1)
                        if mid:
                            s, n = t.slot(2), t.value() + 1
                            dve.wait_ge(tpv_full, n)
                            dve.wait_ge(pair_free, front_use(t, WV) + 1)
                            v.tensor_tensor(vv[:, s, :], tpv[:, :], wv[:, s, :], ALU.mult).then_inc(v_done, 1)
                            dve.wait_ge(a_full, n)
                            dve.wait_ge(n_in[t.slot(UN)], 16 * (t.turn(UN) + 1))
                            if old(t, 1):
                                dve.wait_ge(mcol_done, n - 1)
                                dve.wait_ge(argd_done, n - 1)
                            v.tensor_tensor_scan(mx[:, s, 1:CH + 1], nm[:, t.slot(UN), :], abank[:, :], mx[:, s, 0:1],
                                                 ALU.add, ALU.max).then_inc(m_done, 1)
                            dve.wait_ge(m_done, n)
                            if old(t, 2):
                                dve.wait_ge(prob2_done, n - 2)
                            v.tensor_tensor(argp[:, s, :], abank[:, :], mx[:, s, 1:CH + 1], ALU.subtract).then_inc(argp_done, 1)
                            v.tensor_copy(mx[:, 1 - s, 0:1], mx[:, s, CH:CH + 1]).then_inc(mcol_done, 1)

                    steps(dve, step)

                @block.tensor
                def _(pe):
                    def take(t, k):
                        n = use(t, k)
                        if not (isinstance(t.i, int) and n < 2):
                            pe.wait_ge(pair_free, n - 1)
                        return pair[k % 2]

                    def old(c, by):
                        return not (isinstance(c.i, int) and c.value() < by)

                    def step(t, front, mid, rear, find, count):
                        c = t + 1
                        cs = c.slot(2)

                        def spread(j):
                            n = c.value() * ST + j
                            if not (isinstance(c.i, int) and n < 2):
                                pe.wait_ge(z_done, n - 1)
                            nc.tensor.matmul(sbank[(cs + j) % 2][:, :], bs[:, j, :], hp[:, c.slot(UN), :],
                                             start=True, stop=True).then_inc(shb_full, 1)

                        def product(out, o, s, j):
                            hi, lo = chi[:, j, o:o + O], clo[:, j, o:o + O]
                            nc.tensor.matmul(out[:, :], hi, zhi[:, s, j, :], start=(j == 0), stop=False)
                            if j < ST - 1:
                                nc.tensor.matmul(out[:, :], hi, zlo[:, s, j, :], start=False, stop=False)
                                return nc.tensor.matmul(out[:, :], lo, zhi[:, s, j, :], start=False, stop=False)
                            return nc.tensor.matmul(out[:, :], lo[0:D, :], zhi[0:D, s, j, :], start=False, stop=True)

                        if front:
                            bank = take(t, X_)
                            pe.wait_ge(x_in[cs], 16 * TC * (c.turn(2) + 1))
                            for k in range(TC):
                                mm = nc.tensor.transpose(bank[:, k * P:(k + 1) * P], gx[:, cs, k, :], idn[:, :])
                            mm.then_inc(pair_full, 1)
                            bank = take(t, HID)
                            pe.wait_ge(e_in[c.slot(UN)], 16 * (c.turn(UN) + 1))
                            nc.tensor.matmul(bank[:, :], w1[:, :], v2[0:D, c.slot(UN), :],
                                             start=True, stop=True).then_inc(pair_full, 1)
                        if mid:
                            s, n = t.slot(2), t.value() + 1
                            pe.wait_ge(zlo_done, n * 2)
                            if old(t, 1):
                                pe.wait_ge(kq_done, n - 1)
                            for j in range(ST):
                                mm = product(tpk, 0, s, j)
                            mm.then_inc(tpk_full, 1)
                        if front:
                            pe.wait_ge(h_in[c.slot(UN)], 16 * (c.turn(UN) + 1))
                            spread(0)
                            spread(1)
                            bank = take(t, WK)
                            pe.wait_ge(pair_free, use(t, HID) + 1)
                            nc.tensor.matmul(bank[:, :], w2[:, 0, :], hid[:, cs, :], start=True, stop=True)\
                                .then_inc(pair_full, 1)
                        if mid:
                            if old(t, 1):
                                pe.wait_ge(v_done, n - 1)
                            for j in range(ST):
                                mm = product(tpv, O, s, j)
                                if front and 1 <= j <= 3:
                                    spread(j + 1)
                            mm.then_inc(tpv_full, 1)
                        elif front:
                            for j in range(2, ST):
                                spread(j)
                        if front:
                            bank = take(t, WV)
                            nc.tensor.matmul(bank[:, :], w2[:, 1, :], hid[:, cs, :], start=True, stop=True)\
                                .then_inc(pair_full, 1)
                            pe.wait_ge(q_in[cs], 16 * TC * (c.turn(2) + 1))
                            if old(c, 1):
                                pe.wait_ge(wkq_done, c.value())
                            for k in range(TC):
                                mm = nc.tensor.transpose(qbank[:, k * P:(k + 1) * P], gq[:, cs, k, :], idn[:, :])
                            mm.then_inc(q_full, 1)
                        if mid:
                            pe.wait_ge(kq_done, n)
                            if old(t, 1):
                                pe.wait_ge(argp_done, n - 1)
                            nc.tensor.matmul(abank[:, :], hs[:, :], kq[:, s, :], start=True, stop=True)\
                                .then_inc(a_full, 1)
                        if rear:
                            b = t + (-1)
                            s, n = b.slot(2), b.value() + 1
                            pe.wait_ge(n2_done, n)
                            for half, k in enumerate((ROWA, ROWB)):
                                bank = take(t, k)
                                for m in range(2):
                                    e0 = (2 * half + m) * P
                                    nc.tensor.transpose(bank[:, 256 * m:256 * m + O], n1[:, s, e0:e0 + P], idn[:, :])
                                    mm = nc.tensor.transpose(bank[:, 256 * m + O:256 * m + RW], n2[:, s, e0:e0 + P],
                                                             idn[0:D + H, 0:D + H])
                                mm.then_inc(pair_full, 1)

                    steps(pe, step)

        with ExitStack() as fin:
            fs = lambda name, shape, dt=fp32: fin.enter_context(nc.sbuf_tensor(name, shape, dt))
            xp = fs("xp", [P, HC])
            o0 = fs("o0", [P, HC])
            ag = fs("ag", [P, HC])
            tmpc = fs("tmpc", [P, 4, NT + 1])
            lasti = fs("lasti", [P, 2, NT // 2], i32)
            some = fs("some", [P, 2, NT // 2])
            inv = fs("inv", [P, 2, NT // 2])
            st = fs("st", [P, 10])
            parts = fs("parts", [P, 5])

            each = lambda name, n: [sem(f"{name}{i}") for i in range(n)]
            g_l, y_s = each("rows_gathered", G), each("y_stored", GN)
            xp_in, last_made, counts_made = sem("xp_in"), sem("last_made"), sem("counts_made")
            av_zero = sem("av_zero")
            lslot_made, den_ok, rec_made, rec_some, up_made, av_made = (
                sem("lslot_made"), sem("den_ok"), sem("rec_made"), sem("rec_some"), sem("up_made"), sem("av_made"))
            upT_made, upT_copied, avT_made, avT_copied, o0_made, o0_copied = (
                sem("upT_made"), sem("upT_copied"), sem("avT_made"), sem("avT_copied"), sem("o0_made"), sem("o0_copied"))
            st_d, st_a, st_pe = sem("stats_dve"), sem("stats_act"), sem("stats_pe")
            SS = {k: sem(f"{k}_made") for k in ("r", "y", "mean", "dd", "sq", "var", "lg", "rs", "x1", "z0", "h0", "z1",
                                                "h1", "z2", "y2", "mean2", "dd2", "sq2", "var2", "lg2", "rs2", "o")}

            with ExitStack() as fin1:
                f1 = lambda name, shape, dt=fp32: fin1.enter_context(nc.sbuf_tensor(name, shape, dt))
                lslot = f1("lslot", [P, G, TC], i32)
                gr = f1("gr", [P, G, TC, RW])
                rec = f1("rec", [P, G, 3, TC * H])
                up = f1("up", [P, G, TC, O])
                av = f1("av", [P, G, 2, 2, D])
                upT = f1("upT", [P, G, CH])
                W1C = 2 * P

                def cols(i, j):
                    return bass.ds(i * G * W1C + j * W1C, W1C)

                def tiles(i, j):
                    return bass.ds(i * G * 2 + j * 2, 2)

                with nc.Block() as block:
                    @block.sync
                    def _(sp):
                        sp.dma_start(xp[:, :], xP).then_inc(xp_in, 16)
                        sp.wait_ge(xp_in, 16)

                    @block.gpsimd
                    def _(pool):
                        pool.wait_ge(last_made, 1)

                        def turn(i):
                            for j in range(G):
                                if past(i):
                                    pool.wait_ge(av_made, i * G)
                                    pool.sem_inc(pool_passed, 1)
                                nc.gpsimd.tensor_copy(lslot[:, j, :].rearrange("p (h t) -> p h t", h=2),
                                                      lasti[:, :, tiles(i, j)]).then_inc(lslot_made, 1)
                                pool.wait_ge(lslot_made, i * G + (j + 1))
                                pool.sem_inc(pool_passed, 1)
                                for k in range(TC):
                                    nc.gpsimd.indirect_dma_start(
                                        out=gr[:, j, k, :], out_offset=None, in_=rows[:, :],
                                        in_offset=bass.IndirectOffsetOnAxis(ap=lslot[:, j, k:k + 1], axis=0),
                                    ).then_inc(g_l[j], 16)

                        turns_of(pool, NB // G, turn)

                    @block.tensor
                    def _(pe):
                        t = nc.tensor
                        pe.wait_ge(xp_in, 16)

                        def turn(i):
                            for j in range(G):
                                pe.wait_ge(up_made, i * G + (j + 1))
                                if past(i):
                                    pe.wait_ge(o0_copied, i * G)
                                for k in range(TC):
                                    mm = t.transpose(banks[j][:, k * P:(k + 1) * P], up[:, j, k, :], idn[:, :])
                                mm.then_inc(upT_made, 1)
                            for j in range(G):
                                pe.wait_ge(upT_copied, i * G + (j + 1))
                                pe.wait_ge(av_made, i * G + (j + 1))
                                for k in range(2):
                                    mm = t.transpose(banks[j][:, k * P:(k + 1) * P],
                                                     av[:, j, k, :, :].rearrange("p h d -> p (h d)"), idn[:, :])
                                mm.then_inc(avT_made, 1)
                            for j in range(G):
                                pe.wait_ge(avT_copied, i * G + (j + 1))
                                out0 = banks[j][:, 0:W1C]
                                t.matmul(out0, wself[:, :], xp[:, cols(i, j)], start=True, stop=False)
                                t.matmul(out0, wout[:, 0, :], upT[:, j, 0:W1C], start=False, stop=False)
                                t.matmul(out0, wout[:, 1, :], upT[:, j, W1C:2 * W1C], start=False, stop=True)\
                                    .then_inc(o0_made, 1)

                        turns_of(pe, NB // G, turn)

                    @block.scalar
                    def _(act):
                        f = nc.scalar.activation

                        def turn(i):
                            for j in range(G):
                                act.wait_ge(upT_made, i * G + (j + 1))
                                f(upT[:, j, :], banks[j][:, :], ACT.Copy).then_inc(upT_copied, 1)
                            for j in range(G):
                                act.wait_ge(avT_made, i * G + (j + 1))
                                f(ag[:, cols(i, j)], banks[j][:, 0:W1C], ACT.Copy).then_inc(avT_copied, 1)
                            for j in range(G):
                                act.wait_ge(o0_made, i * G + (j + 1))
                                f(o0[:, cols(i, j)], banks[j][:, 0:W1C], ACT.Copy).then_inc(o0_copied, 1)

                        turns_of(act, NB // G, turn)

                    @block.vector
                    def _(dve):
                        v = nc.vector
                        flat = lambda a: a[:, :, :].rearrange("p h t -> p (h t)")
                        v.tensor_scalar(tmpc[:, 0, :], rowc[:, :], SR / 2.0, SR * SR / 2.0 + SR / 2.0, ALU.mult, ALU.add)\
                            .then_inc(counts_made, 1)
                        dve.wait_ge(counts_made, 1)
                        v.scalar_tensor_tensor(out=tmpc[:, 1, :], in0=inrow[:, :], scalar=0.5, in1=tmpc[:, 0, :],
                                               op0=ALU.mult, op1=ALU.add).then_inc(counts_made, 1)
                        dve.wait_ge(counts_made, 2)
                        v.tensor_scalar(tmpc[:, 2, 0:NT], tmpc[:, 1, 1:NT + 1], -1.0, 0.0, ALU.add, ALU.max)\
                            .then_inc(counts_made, 1)
                        dve.wait_ge(counts_made, 3)
                        v.tensor_copy(flat(lasti), tmpc[:, 2, 0:NT]).then_inc(last_made, 1)
                        v.tensor_tensor(flat(inv), tmpc[:, 1, 1:NT + 1], tmpc[:, 1, 0:NT], ALU.subtract).then_inc(counts_made, 1)
                        dve.wait_ge(counts_made, 4)
                        v.tensor_scalar(flat(some), flat(inv), 1.0, None, ALU.min).then_inc(counts_made, 1)
                        v.tensor_scalar(tmpc[:, 3, 0:NT], flat(inv), 1.0, None, ALU.max).then_inc(counts_made, 1)
                        dve.wait_ge(counts_made, 6)
                        v.reciprocal(tmpc[:, 0, 0:NT], tmpc[:, 3, 0:NT]).then_inc(counts_made, 1)
                        dve.wait_ge(counts_made, 7)
                        v.tensor_tensor(flat(inv), tmpc[:, 0, 0:NT], flat(some), ALU.mult).then_inc(counts_made, 1)
                        dve.wait_ge(counts_made, 8)

                        def turn(i):
                            for j in range(G):
                                n = i * G + (j + 1)
                                dve.wait_ge(g_l[j], i * 16 * TC + 16 * TC)
                                rv = [rec[:, j, q, :].rearrange("p (t h) -> p t h", h=H) for q in range(3)]
                                four = lambda a: a.rearrange("p (a t) h -> p a t h", a=2)
                                v.tensor_scalar(rv[0], gr[:, j, :, O + D:RW], 1e-16, None, ALU.add).then_inc(den_ok, 1)
                                dve.wait_ge(den_ok, n)
                                v.reciprocal(rv[1], rv[0]).then_inc(rec_made, 1)
                                dve.wait_ge(rec_made, n)
                                v.tensor_tensor(four(rv[2]), four(rv[1]),
                                                some[:, :, tiles(i, j)].unsqueeze(3).broadcast_to([P, 2, 2, H]),
                                                ALU.mult).then_inc(rec_some, 1)
                                dve.wait_ge(rec_some, n)
                                if past(i):
                                    dve.wait_ge(avT_made, i * G)
                                v.tensor_tensor(up[:, j, :, :].rearrange("p t (d h) -> p t d h", h=H),
                                                gr[:, j, :, 0:O].rearrange("p t (d h) -> p t d h", h=H),
                                                rv[2].unsqueeze(2).broadcast_to([P, TC, DH, H]), ALU.mult).then_inc(up_made, 1)
                                v.tensor_tensor(av[:, j, :, :, :].rearrange("p t h d -> p h t d"),
                                                gr[:, j, :, O:O + D].rearrange("p (h t) d -> p h t d", h=2),
                                                inv[:, :, tiles(i, j)].unsqueeze(3).broadcast_to([P, 2, 2, D]),
                                                ALU.mult).then_inc(av_made, 1)

                        turns_of(dve, NB // G, turn)

            with ExitStack() as fin2:
                f2 = lambda name, shape, dt=fp32: fin2.enter_context(nc.sbuf_tensor(name, shape, dt))
                junk = f2("junk", [P, 10 * ROWS_OK], bf16)
                work = {k: f2(f"{k}_", [P, GN, CN]) for k in ("r", "y", "dd", "sq", "lg", "rs", "x1")}
                work |= {"h0": work["r"], "y2": work["r"], "h1": work["y"]}
                W = lambda k, j: work[k][:, j, :]
                bank_of = lambda j: banks[j][:, 0:CN]

                def ncols(i, j):
                    return bass.ds(i * GN * CN + j * CN, CN)

                with nc.Block() as block:
                    @block.sync
                    def _(sp):
                        def turn(i):
                            for j in range(GN):
                                sp.wait_ge(SS["o"], i * GN + (j + 1))
                                sp.dma_start(out[:, ncols(i, j)], W("sq", j)).then_inc(y_s[j], 16)

                        turns_of(sp, NN // GN, turn)
                        for j in range(GN):
                            sp.wait_ge(y_s[j], 16 * (NN // GN))

                    @block.tensor
                    def _(pe):
                        t = nc.tensor
                        for k in range(2):
                            pe.wait_ge(st_d, 1 + 2 * k)
                            t.matmul(banks[k][:, 0:2], fold[:, :], st[:, 2 * k:2 * k + 2], start=True, stop=True).then_inc(st_pe, 1)

                        def product(name, lhsT, after, src, i):
                            for j in range(GN):
                                pe.wait_ge(SS[after], i * GN + (j + 1))
                                t.matmul(bank_of(j), lhsT[:, :], W(src, j), start=True, stop=True).then_inc(SS[name], 1)

                        def turn(i):
                            product("mean", mn, "y", "y", i)
                            product("var", mn, "sq", "sq", i)
                            for j in range(GN):
                                pe.wait_ge(SS["x1"], i * GN + (j + 1))
                                t.matmul(bank_of(j), m0e[:, :], ag[:, ncols(i, j)], start=True, stop=False)
                                t.matmul(bank_of(j), m0x[:, :], W("x1", j), start=False, stop=True).then_inc(SS["z0"], 1)
                            product("z1", m1, "h0", "h0", i)
                            product("z2", m2, "h1", "h1", i)
                            product("mean2", mn, "y2", "y2", i)
                            product("var2", mn, "sq2", "sq", i)

                        turns_of(pe, NN // GN, turn)

                    @block.scalar
                    def _(act):
                        f = nc.scalar.activation
                        act.wait_ge(st_d, 2)
                        ov = o0[:, :].rearrange("d (t p) -> d t p", p=P)
                        for q in range(5):
                            if q:
                                act.wait_ge(st_a, q)
                            f(junk[:, :].rearrange("d (t p) -> d t p", p=ROWS_OK), ov[:, 10 * q:10 * q + 10, 0:ROWS_OK],
                              ACT.Square, bias=st[:, 4:5], accum_out=parts[:, q:q + 1]).then_inc(st_a, 1)
                        act.wait_ge(st_pe, 2)
                        f(st[:, 5:6], banks[1][:, 0:1], ACT.Ln, bias=epsc[:, 0:1], scale=1.0 / N).then_inc(st_a, 1)
                        act.wait_ge(st_a, 6)
                        f(st[:, 6:7], st[:, 5:6], ACT.Exp, scale=-0.5).then_inc(st_a, 1)

                        def each_block(name, after, fn, i):
                            for j in range(GN):
                                act.wait_ge(SS[after], i * GN + (j + 1))
                                fn(j).then_inc(SS[name], 1)

                        act.wait_ge(st_d, 6)

                        def turn(i):
                            for j in range(GN):
                                if past(i):
                                    act.wait_ge(SS["o"], i * GN)
                                f(W("r", j), xp[:, ncols(i, j)], ACT.Identity, bias=st[:, 9:10]).then_inc(SS["r"], 1)
                            for j in range(GN):
                                if past(i):
                                    act.wait_ge(y_s[j], i * 16)
                                act.wait_ge(SS["dd"], i * GN + (j + 1))
                                f(W("sq", j), W("dd", j), ACT.Square).then_inc(SS["sq"], 1)
                            each_block("lg", "var", lambda j: f(W("lg", j), bank_of(j), ACT.Ln, bias=epsc[:, 0:1]), i)
                            each_block("rs", "lg", lambda j: f(W("rs", j), W("lg", j), ACT.Exp, scale=-0.5), i)
                            each_block("h0", "z0", lambda j: f(W("h0", j), bank_of(j), ACT.Relu, bias=mb[:, 0:1]), i)
                            each_block("h1", "z1", lambda j: f(W("h1", j), bank_of(j), ACT.Relu, bias=mb[:, 1:2]), i)
                            each_block("sq2", "dd2", lambda j: f(W("sq", j), W("dd", j), ACT.Square), i)
                            each_block("lg2", "var2", lambda j: f(W("lg", j), bank_of(j), ACT.Ln, bias=epsc[:, 0:1]), i)
                            each_block("rs2", "lg2", lambda j: f(W("rs", j), W("lg", j), ACT.Exp, scale=-0.5), i)

                        turns_of(act, NN // GN, turn)

                    @block.vector
                    def _(dve):
                        v = nc.vector
                        v.memset(st[:, :], 0.0).then_inc(av_zero, 1)
                        dve.wait_ge(av_zero, 1)
                        ov = o0[:, :].rearrange("d (t p) -> d t p", p=P)[:, :, 0:ROWS_OK]
                        v.tensor_reduce(st[:, 0:1], ov, AX.XY, ALU.add).then_inc(st_d, 1)
                        dve.wait_ge(st_pe, 1)
                        v.tensor_scalar(st[:, 4:5], banks[0][:, 0:1], -1.0 / N, None, ALU.mult).then_inc(st_d, 1)
                        dve.wait_ge(st_a, 5)
                        v.tensor_reduce(st[:, 2:3], parts[:, :], AX.X, ALU.add).then_inc(st_d, 1)
                        dve.wait_ge(st_a, 7)
                        v.tensor_tensor(st[:, 7:8], st[:, 6:7], gb[:, 0:1], ALU.mult).then_inc(st_d, 1)
                        dve.wait_ge(st_d, 4)
                        v.tensor_tensor(st[:, 8:9], st[:, 7:8], st[:, 4:5], ALU.mult).then_inc(st_d, 1)
                        dve.wait_ge(st_d, 5)
                        v.tensor_tensor(st[:, 9:10], st[:, 8:9], gb[:, 1:2], ALU.add).then_inc(st_d, 1)

                        def each_block(name, after, fn, i):
                            for j in range(GN):
                                dve.wait_ge(SS[after], i * GN + (j + 1))
                                fn(j).then_inc(SS[name], 1)

                        def turn(i):
                            each_block("y", "r", lambda j: v.scalar_tensor_tensor(
                                out=W("y", j), in0=o0[:, ncols(i, j)], scalar=st[:, 7:8], in1=W("r", j),
                                op0=ALU.mult, op1=ALU.add), i)
                            each_block("dd", "mean", lambda j: v.tensor_tensor(W("dd", j), W("y", j), bank_of(j), ALU.subtract), i)
                            each_block("x1", "rs", lambda j: v.tensor_tensor(W("x1", j), W("dd", j), W("rs", j), ALU.mult), i)
                            each_block("y2", "z2", lambda j: v.scalar_tensor_tensor(
                                out=W("y2", j), in0=bank_of(j), scalar=mb[:, 2:3], in1=W("x1", j),
                                op0=ALU.add, op1=ALU.add), i)
                            each_block("dd2", "mean2", lambda j: v.tensor_tensor(W("dd", j), W("y2", j), bank_of(j),
                                                                                 ALU.subtract), i)
                            each_block("o", "rs2", lambda j: v.tensor_tensor(W("sq", j), W("dd", j), W("rs", j), ALU.mult), i)

                        turns_of(dve, NN // GN, turn)


def kernel(**inputs):
    import numpy as np
    import concourse.bacc as bacc
    import ml_dtypes
    from concourse.bass_utils import run_bass_kernel_spmd

    g = {k: np.asarray(v) for k, v in inputs.items()}
    hd = lambda w: np.ascontiguousarray(w.reshape(w.shape[:-1] + (H, DH)).swapaxes(-1, -2).reshape(w.shape))
    pad_e = lambda v, fill: np.concatenate([v, np.full(EP - E, fill, v.dtype)])
    tiles = lambda v: pad_e(v, 0).reshape(NC, TC, P).transpose(2, 0, 1)
    col = lambda v: v.reshape(-1, 1)
    none = np.zeros((D, D), np.float32)
    twice = lambda w: np.block([[w, none], [none, w]])
    both_rows = lambda *v: np.stack([np.concatenate([a, a]) for a in v], axis=1)

    x = g["x"]
    xT = np.zeros((D, NT, P), x.dtype)
    xT[:, :, :ROWS_OK] = x.reshape(ROWS_OK, NT, D).transpose(2, 1, 0)
    both = np.concatenate([hd(g["L0_gnn_Cqk"]), hd(g["L0_gnn_Cv"])], axis=-1)
    ctp = np.zeros((2, D, ST, 2 * O), both.dtype)
    for s in range(S):
        ctp[s % 2, :, s // 2] = both[:, s]
    ctp[1, :, ST - 1] = both[:, S - 1]
    shT = np.zeros((S, EP), np.float32)
    shT[:, :E] = g["edge_attr_9"].T
    eT = np.zeros((D, EP), np.float32)
    eT[:, :E] = g["edge_attr_64"].T

    bsel = np.zeros((3, S, ST, P), np.float32)
    for s in range(S):
        bsel[:, s, s // 2, (s % 2) * D:(s % 2 + 1) * D] = 1
    bsel[:, S - 1, ST - 1, :] = 1
    hsel = (np.arange(P)[:, None] % H == np.arange(P)[None, :] % H).astype(np.float32)

    wout = g["L0_gnn_W_out"].reshape(H, DH, D).transpose(1, 0, 2).reshape(O, D)
    arrays = {
        "xg": np.concatenate([x, x], axis=1), "xT": xT.reshape(D, NP),
        "idx": np.concatenate([tiles(g["src"]), tiles(g["dst"])], axis=2).reshape(P, NC * 2 * TC),
        "dnow": pad_e(g["dst"], NP), "dbefore": np.concatenate([np.full(1, -1, np.int32), pad_e(g["dst"], NP)[:-1]]),
        "shT": shT, "eT": eT, "Wq": hd(g["L0_gnn_Wq"]), "Ctp": ctp.reshape(P, ST, 2 * O),
        "W1": np.concatenate([g["L0_gnn_k_w1"], g["L0_gnn_v_w1"]], axis=1),
        "b1": col(np.concatenate([g["L0_gnn_k_b1"], g["L0_gnn_v_b1"]])),
        "Wk2": hd(g["L0_gnn_k_w2"]), "Wv2": hd(g["L0_gnn_v_w2"]),
        "b2": np.stack([hd(g["L0_gnn_k_b2"]), hd(g["L0_gnn_v_b2"])], axis=1),
        "Wout": np.stack([np.concatenate([wout, np.zeros_like(wout)], axis=1), np.concatenate([np.zeros_like(wout), wout], axis=1)], axis=1),
        "Wself": twice(g["L0_gnn_W_self"]), "gamma_beta": both_rows(g["L0_gnn_gamma"], g["L0_gnn_beta"]),
        "M0e": twice(g["L1_gnn_W0"][:D]), "M0x": twice(g["L1_gnn_W0"][D:]), "M1": twice(g["L1_gnn_W1"]),
        "M2": twice(g["L1_gnn_W2"]), "mbias": both_rows(g["L1_gnn_b0"], g["L1_gnn_b1"], g["L1_gnn_b2"]),
        "bsel": bsel.reshape(3 * S, ST, P).astype(ml_dtypes.bfloat16), "hsel": hsel,
        "ident": np.eye(P, dtype=np.float32), "mean64": twice(np.full((D, D), 1.0 / D, np.float32)),
        "halves": np.tile(np.eye(D, dtype=np.float32), (2, 2)),
        "xP": xT.reshape(D, 2, HC).transpose(1, 0, 2).reshape(P, HC),
    }
    arrays = {f"in_{k}": np.ascontiguousarray(v) for k, v in arrays.items()}
    nc = bacc.Bacc("TRN2", target_bir_lowering=False, num_devices=1)
    args = [nc.dram_tensor(k, v.shape, mybir.dt.from_np(v.dtype), kind="ExternalInput").ap() for k, v in arrays.items()]
    res = nc.dram_tensor("out_y", (P, HC), fp32, kind="ExternalOutput").ap()
    gnn_kernel(nc, *args, res)
    r = run_bass_kernel_spmd(nc, [arrays], core_ids=[0])
    y = r.results[0]["out_y"].reshape(2, D, HC).transpose(1, 0, 2).reshape(D, NT, P)[:, :, :ROWS_OK]
    return np.ascontiguousarray(y.transpose(2, 1, 0).reshape(N, D))
```

```python
from contextlib import ExitStack

import concourse.bass as bass
from concourse import mybir

fp32 = mybir.dt.float32
f32r = mybir.dt.float32r
bf16 = mybir.dt.bfloat16
i32 = mybir.dt.int32
ALU = mybir.AluOpType
ACT = mybir.ActivationFunctionType
AX = mybir.AxisListType

P = 128
N, E, D, S, H, DH = 12500, 200000, 64, 9, 8, 16
O = H * DH
CH = 512
TC = CH // P
UN = 4
NC = -(-E // (CH * UN)) * UN
EP = NC * CH
EC = EP // P
NT = 100
NP = NT * P
NB = NT // TC
G = 5
HC = NP // 2
NN, GN = 16, 8
CN = HC // NN
ROWS_OK = N // NT
SR = 448
ST = (S + 1) // 2
RW = O + D + H
BIG = 1e30
EPS = 1e-5
TURNS = (NC - 6) // UN
assert TURNS <= NT + 1 <= TURNS + NC + 1 - 3 - UN * TURNS
assert SR * SR == EP and ROWS_OK * NT == N and NT % TC == 0


class Chunk:

    def __init__(self, i, r):
        self.i, self.r = i, r

    def __add__(self, k):
        return Chunk(self.i, self.r + k)

    def value(self):
        return self.i * UN + self.r

    def slot(self, n):
        return self.r % n

    def turn(self, n):
        return self.i * (UN // n) + self.r // n


def past(i):
    return not isinstance(i, int) or i > 0


def turns_of(engine, n, turn):
    turn(0)
    with engine.Fori(1, n) as i:
        turn(i)


def gnn_kernel(nc, xg, xT, idx, dnow, dbefore, dlast, shT, eT, Wq, Ctp, W1, b1, Wk2, Wv2, b2, Wout, Wself, gamma_beta,
               M0e, M0x, M1, M2, mbias, bsel, hsel, ident, mean64, halves, xP, out):
    dram = lambda name, shape, dt: nc.dram_tensor(name, shape, dt, kind="Internal").ap()
    qtab = dram("qtab", (NP, O), fp32)
    newd = dram("newd", (EP,), bf16)
    shp = dram("shp", (3, S * EP), bf16)
    rows = dram("rows", (EP, RW), fp32)

    ctx = ExitStack()
    with ctx:
        def sb(name, shape, dt=fp32):
            return ctx.enter_context(nc.sbuf_tensor(name, shape, dt))

        def pb(name, shape, dt=fp32):
            return ctx.enter_context(nc.psum_tensor(name, shape, dt))

        def sem(name):
            return ctx.enter_context(nc.semaphore(name))

        wq = sb("wq", [D, O])
        chi = sb("chi", [P, ST, 2 * O], f32r)
        clo = sb("clo", [P, ST, 2 * O], f32r)
        w1 = sb("w1", [D, P])
        b1c = sb("b1c", [P, 1])
        w2hi = sb("w2hi", [P, 2, O], f32r)
        w2lo = sb("w2lo", [P, 2, O], f32r)
        b2c = sb("b2c", [P, 2])
        wout = sb("wout", [O, 2, P])
        wself = sb("wself", [P, P])
        m0e = sb("m0e", [P, P])
        m0x = sb("m0x", [P, P])
        m1 = sb("m1", [P, P])
        m2 = sb("m2", [P, P])
        mn = sb("mn", [P, P])
        fold = sb("fold", [P, P])
        gb = sb("gb", [P, 2])
        mb = sb("mb", [P, 3])
        bs = sb("bs", [3 * S, ST, P], bf16)
        hs = sb("hs", [P, P], f32r)
        idn = sb("idn", [P, P])
        epsc = sb("epsc", [P, 1])
        idx_all = sb("idx_all", [P, 2 * EC], i32)
        nodeh = sb("nodeh", [P, NT + 1])
        rowc = sb("rowc", [P, NT + 1])
        inrow = sb("inrow", [P, NT + 1])

        banks = [pb(f"bank{i}", [P, 512]) for i in range(8)]

        load = sem("load")
        pool_passed, sp_passed, act_passed = sem("pool_passed"), sem("sp_passed"), sem("act_passed")
        with ExitStack() as prep:
            ps = lambda name, shape, dt=fp32: prep.enter_context(nc.sbuf_tensor(name, shape, dt))
            ctp = ps("ctp", [P, ST, 2 * O])
            w2 = ps("w2", [P, 2, O])
            hsin = ps("hsin", [P, P])
            xq = ps("xq", [D, G, CH])
            qs = ps("qs", [P, G, TC, O])
            dcur = ps("dcur", [P, EC], i32)
            dprv = ps("dprv", [P, EC], i32)
            same = ps("same", [P, EC])
            neg = ps("neg", [P, EC], bf16)
            nodei = ps("nodei", [P, NT + 1], i32)
            shin = ps("shin", [P, 3, EC])
            shr = ps("shr", [P, 2, EC])
            parts3 = ps("parts3", [P, 3, 3, EC], bf16)

            dst_in, weights_in, w2_zero, nodes_made = sem("dst_in"), sem("weights_in"), sem("w2_zero"), sem("nodes_made")
            w_split, neg_made, neg_stored = sem("w_split"), sem("neg_made"), sem("neg_stored")
            sh_in = [sem(f"sh_in{i}") for i in range(3)]
            sh_out = [sem(f"sh_out{i}") for i in range(3)]
            first_made, rest_made, second_made, third_made = (
                sem("first_made"), sem("rest_made"), sem("second_made"), sem("third_made"))
            q_made, q_copied = sem("q_made"), sem("q_copied")
            xq_in = [sem(f"xq_in{i}") for i in range(G)]
            q_out = [sem(f"q_out{i}") for i in range(G)]
            wq_in = sem("wq_in")

            with nc.Block() as block:
                @block.sync
                def _(sp):
                    def harmonic_in(s):
                        if s >= 3:
                            sp.wait_ge(third_made, s - 2)
                        sp.dma_start(shin[:, s % 3, :], shT[s].rearrange("(p c) -> p c", p=P)).then_inc(sh_in[s % 3], 16)

                    sp.dma_start(wq[:, :], Wq).then_inc(wq_in, 16)
                    harmonic_in(0)
                    harmonic_in(1)
                    sp.dma_start(dcur[:, :], dnow.rearrange("(p c) -> p c", p=P)).then_inc(dst_in, 16)
                    sp.dma_start(dprv[:, :], dbefore.rearrange("(p c) -> p c", p=P)).then_inc(dst_in, 16)
                    harmonic_in(2)
                    sp.dma_start(ctp[:, :, :], Ctp).then_inc(weights_in, 16)
                    sp.wait_ge(w2_zero, 1)
                    sp.dma_start(w2[0:D, 0, :], Wk2).then_inc(weights_in, 16)
                    sp.dma_start(w2[D:P, 1, :], Wv2).then_inc(weights_in, 16)
                    sp.dma_start(hsin[:, :], hsel).then_inc(weights_in, 16)
                    consts = ((w1[:, :], W1), (b1c[:, :], b1), (b2c[:, :], b2), (wout[:, :, :], Wout),
                              (wself[:, :], Wself), (gb[:, :], gamma_beta), (m0e[:, :], M0e), (m0x[:, :], M0x),
                              (m1[:, :], M1), (m2[:, :], M2), (mb[:, :], mbias), (bs[:, :, :], bsel),
                              (idn[:, :], ident), (mn[:, :], mean64), (fold[:, :], halves),
                              (idx_all[:, :], idx))
                    for dst, src in consts:
                        sp.dma_start(dst, src).then_inc(load, 16)
                    for s in range(S):
                        sp.wait_ge(third_made, s + 1)
                        dst = shp[:, s * EP:(s + 1) * EP].rearrange("j (p c) -> p j c", p=P)
                        sp.dma_start(dst, parts3[:, s % 3, :, :]).then_inc(sh_out[s % 3], 16)
                        if s + 3 < S:
                            harmonic_in(s + 3)
                    sp.wait_ge(neg_made, 2)
                    sp.dma_start(newd.rearrange("(p c) -> p c", p=P), neg[:, :]).then_inc(neg_stored, 16)
                    sp.wait_ge(load, 16 * len(consts))
                    sp.wait_ge(neg_stored, 16)
                    for k in range(3):
                        sp.wait_ge(sh_out[k], 16 * (S // 3))

                @block.tensor
                def _(pe):
                    pe.wait_ge(wq_in, 16)

                    def turn(i):
                        for j in range(G):
                            pe.wait_ge(xq_in[j], i * 16 + 16)
                            if past(i):
                                pe.wait_ge(q_copied, (i - 1) * G + (j + 1))
                            for k in range(TC):
                                mm = nc.tensor.matmul(banks[j][:, k * O:(k + 1) * O], xq[:, j, k * P:(k + 1) * P],
                                                      wq[:, :], start=True, stop=True)
                            mm.then_inc(q_made, 1)

                    turns_of(pe, NB // G, turn)

                @block.scalar
                def _(act):
                    view = qtab.rearrange("(p t) o -> p t o", t=NT)

                    def x_in_block(i, j):
                        act.dma_start(xq[:, j, :], xT[:, bass.ds(i * G * CH + j * CH, CH)]).then_inc(xq_in[j], 16)

                    def turn(i, more=True):
                        for j in range(G):
                            n = i * G + (j + 1)
                            act.wait_ge(q_made, n)
                            if more:
                                x_in_block(i + 1, j)
                            if past(i):
                                act.wait_ge(q_out[j], i * 16)
                            nc.scalar.activation(qs[:, j, :, :], banks[j][:, :].rearrange("p (t o) -> p t o", t=TC),
                                                 ACT.Copy).then_inc(q_copied, 1)
                            act.wait_ge(q_copied, n)
                            act.dma_start(view[:, bass.ds(i * G * TC + j * TC, TC), :], qs[:, j, :, :]).then_inc(q_out[j], 16)

                    for j in range(G):
                        x_in_block(0, j)
                    last = NB // G - 1
                    turns_of(act, last, turn)
                    turn(last, more=False)
                    for j in range(G):
                        act.wait_ge(q_out[j], 16 * (NB // G))

                @block.gpsimd
                def _(pool):
                    nc.gpsimd.iota(nodei[:, :], pattern=[[1, NT + 1]], base=-1,
                                   channel_multiplier=NT).then_inc(nodes_made, 1)

                @block.vector
                def _(dve):
                    v = nc.vector
                    v.memset(w2[:, :, :], 0.0).then_inc(w2_zero, 1)
                    v.memset(epsc[:, :], EPS)
                    dve.wait_ge(nodes_made, 1)
                    v.tensor_scalar(nodeh[:, :], nodei[:, :], 0.5, None, ALU.add)
                    for s in range(S + 1):
                        if s < S:
                            dve.wait_ge(sh_in[s % 3], 16 * (s // 3 + 1))
                            if s >= 3:
                                dve.wait_ge(sh_out[s % 3], 16 * (s // 3))
                            v.tensor_copy(parts3[:, s % 3, 0, :], shin[:, s % 3, :]).then_inc(first_made, 1)
                        if s >= 1:
                            k = s - 1
                            dve.wait_ge(rest_made, k + 1)
                            v.tensor_copy(parts3[:, k % 3, 1, :], shr[:, k % 2, :]).then_inc(second_made, 1)
                        if s < S:
                            dve.wait_ge(first_made, s + 1)
                            if s >= 2:
                                dve.wait_ge(third_made, s - 1)
                            v.tensor_tensor(shr[:, s % 2, :], shin[:, s % 3, :], parts3[:, s % 3, 0, :],
                                            ALU.subtract).then_inc(rest_made, 1)
                        if s >= 1:
                            dve.wait_ge(second_made, k + 1)
                            v.tensor_tensor(parts3[:, k % 3, 2, :], shr[:, k % 2, :], parts3[:, k % 3, 1, :],
                                            ALU.subtract).then_inc(third_made, 1)
                        if s == 1:
                            dve.wait_ge(dst_in, 16 * 2)
                            v.tensor_tensor(same[:, :], dcur[:, :], dprv[:, :], ALU.is_equal).then_inc(neg_made, 1)
                            dve.wait_ge(neg_made, 1)
                            v.tensor_scalar(neg[:, :], same[:, :], 1.0, BIG, ALU.subtract, ALU.mult).then_inc(neg_made, 1)
                        if s == 3:
                            dve.wait_ge(weights_in, 16 * 4)
                            v.tensor_copy(chi[:, :, :], ctp[:, :, :]).then_inc(w_split, 1)
                            v.tensor_copy(w2hi[:, :, :], w2[:, :, :]).then_inc(w_split, 1)
                            v.tensor_copy(hs[:, :], hsin[:, :])
                            dve.wait_ge(w_split, 2)
                            v.tensor_tensor(clo[:, :, :], ctp[:, :, :], chi[:, :, :].bitcast(fp32), ALU.subtract)
                            v.tensor_tensor(w2lo[:, :, :], w2[:, :, :], w2hi[:, :, :].bitcast(fp32), ALU.subtract)

        with ExitStack() as main:
            ms = lambda name, shape, dt=fp32: main.enter_context(nc.sbuf_tensor(name, shape, dt))
            idxs = ms("idxs", [P, UN, 2 * TC], i32)
            gx = ms("gx", [P, 2, TC, 2 * D])
            gq = ms("gq", [P, 2, TC, O])
            v2 = ms("v2", [D + H, UN, CH])
            hp = ms("hp", [3 * S, UN, CH], bf16)
            nm = ms("nm", [P, UN, CH], bf16)
            xd = ms("xd", [P, 2, CH])
            hid = ms("hid", [P, CH])
            hidhi = ms("hidhi", [P, CH], f32r)
            hidlo = ms("hidlo", [P, CH], f32r)
            wk = ms("wk", [P, 2, CH])
            wv = ms("wv", [P, 2, CH])
            z = ms("z", [P, ST, CH])
            zhi = ms("zhi", [P, 2, ST, CH], f32r)
            zlo = ms("zlo", [P, 2, ST - 1, CH], f32r)
            wkq = ms("wkq", [P, 2, CH])
            kq = ms("kq", [P, CH])
            kqhi = ms("kqhi", [P, CH], f32r)
            kqlo = ms("kqlo", [P, CH], f32r)
            vv = ms("vv", [P, 2, CH])
            mprev = ms("mprev", [P, 2, CH])
            over = ms("over", [P, 2, CH])
            rise = ms("rise", [P, CH])
            below = ms("below", [P, CH])
            prob = ms("prob", [P, 2, CH])
            dec = ms("dec", [P, 2, CH])
            d2 = ms("d2", [D + H, 2, CH])
            pv = ms("pv", [P, 2, CH])
            n1 = ms("n1", [P, 2, CH])
            n2 = ms("n2", [D + H, 2, CH])
            ot = ms("ot", [P, 2, TC, RW])
            lastd = ms("lastd", [P, SR], i32)
            grow = ms("grow", [P, SR], i32)
            rslot = ms("rslot", [P, 1], i32)
            signs = ms("signs", [P, SR], bf16)

            pair = banks[0:2]
            sbank = banks[2:4]
            tpk, tpv, qbank, abank = banks[4:8]

            e_in = [sem(f"edges_in{i}") for i in range(UN)]
            h_in = [sem(f"harmonics_in{i}") for i in range(UN)]
            n_in = [sem(f"newd_in{i}") for i in range(UN)]
            x_in = [sem(f"x_gathered{i}") for i in range(2)]
            q_in = [sem(f"q_gathered{i}") for i in range(2)]
            o_out = [sem(f"rows_stored{i}") for i in range(2)]
            idx_made = sem("idx_made")
            pair_full, pair_free = sem("pair_full"), sem("pair_copied")
            shb_full, z_done, zhi_done, zlo_done = sem("shb_full"), sem("z_done"), sem("zhi_done"), sem("zlo_done")
            tpk_full, tpv_full, q_full, a_full = sem("tpk_full"), sem("tpv_full"), sem("q_full"), sem("attn_full")
            wkq_done, kq_done, v_done = sem("wkq_done"), sem("kq_done"), sem("v_done")
            hidhi_done, hidlo_done, kqhi_done, kqlo_done, zlo0_done = (
                sem("hidhi_done"), sem("hidlo_done"), sem("kqhi_done"), sem("kqlo_done"), sem("zlo0_done"))
            m_done, mcol_done, over_done = sem("max_done"), sem("maxcol_done"), sem("over_done")
            below_done, rise_done = sem("below_done"), sem("rise_done")
            prob_done, dec_done, mask_done = sem("prob_done"), sem("dec_done"), sem("mask_done")
            prob2_in = [sem(f"prob2_in{i}") for i in range(2)]
            dec2_in = [sem(f"dec2_in{i}") for i in range(2)]
            pv_done, n1_done, n2_done = sem("pv_done"), sem("n1_done"), sem("n2_done")
            zeroed = sem("zeroed")
            lastd_in, row_found, row_slot, row_in, row_counted = (
                sem("lastd_in"), sem("row_found"), sem("row_slot"), sem("row_in"), sem("row_counted"))

            X_, HID, WK, WV, ROWA, ROWB = range(6)

            def use(t, k):
                if isinstance(t.i, int):
                    n = t.value()
                    if n <= 0:
                        return 4 * (n + 1) + k
                    if n >= NC - 1:
                        return 6 * (NC - 1) + 2 + 2 * (n - NC + 1) + k - 4
                    return 6 * n + 2 + k
                return t.value() * 6 + 2 + k

            def front_use(c, k):
                return use(c + (-1), k)

            def steps(engine, step):
                def has(n):
                    return n + 1 < NC, 0 <= n < NC, 1 <= n <= NC

                for n in range(-1, 3):
                    step(Chunk(0, n), *has(n), None, None, None)
                with engine.Fori(0, TURNS) as i:
                    for k in range(UN):
                        step(Chunk(i, 3 + k), True, True, True, *(i if k == at else None for at in (0, 1, 3)))
                for n in range(3 + UN * TURNS, NC + 1):
                    m = n - 3 - (UN - 1) * TURNS
                    step(Chunk(0, n), *has(n), *(m if m <= NT else None,) * 2, m - 1 if TURNS <= m - 1 <= NT else None)

            with nc.Block() as block:
                @block.sync
                def _(sp):
                    sp.wait_ge(zeroed, 3)

                    def loads(c):
                        s, t = c.slot(UN), c.turn(UN)
                        at = c.value() * CH
                        old = c + (-UN)
                        first = isinstance(c.i, int) and c.value() < UN
                        if not first:
                            sp.wait_ge(n2_done, old.value() + 1)
                            sp.sem_inc(sp_passed, 1)
                            sp.wait_ge(shb_full, (old.value() + 1) * ST)
                            sp.sem_inc(sp_passed, 1)
                            sp.wait_ge(m_done, old.value() + 1)
                            sp.sem_inc(sp_passed, 1)
                            sp.wait_ge(mask_done, old.value() + 1)
                            sp.sem_inc(sp_passed, 1)
                        sp.dma_start(v2[0:D, s, :], eT[:, bass.ds(at, CH)]).then_inc(e_in[s], 16)
                        part = shp.rearrange("j (s e) -> (j s) e", s=S)
                        sp.dma_start(hp[:, s, :], part[:, bass.ds(at, CH)]).then_inc(h_in[s], 16)
                        sp.dma_start(nm[:, s, :], newd[bass.ds(at, CH)].partition_broadcast(P)).then_inc(n_in[s], 16)

                    def weights_beside(c):
                        s, n = c.slot(2), c.value() + 1
                        sp.wait_ge(prob_done, n)
                        sp.sem_inc(sp_passed, 1)
                        sp.dma_start(v2[D:D + H, c.slot(UN), :], prob[D:D + H, s, :]).then_inc(prob2_in[s], 16)
                        sp.wait_ge(dec_done, n)
                        sp.sem_inc(sp_passed, 1)
                        if not (isinstance(c.i, int) and c.value() < 2):
                            sp.wait_ge(n2_done, n - 2)
                            sp.sem_inc(sp_passed, 1)
                        sp.dma_start(d2[D:D + H, s, :], dec[D:D + H, s, :]).then_inc(dec2_in[s], 16)

                    def store(c):
                        s = c.slot(2)
                        row = use(c + 1, ROWB)
                        sp.wait_ge(pair_free, row + 1)
                        dst = rows[bass.ds(c.value() * CH, CH), :].rearrange("(t p) w -> p t w", p=P)
                        sp.dma_start(dst, ot[:, s, :, :]).then_inc(o_out[s], 16)

                    for n in range(2):
                        loads(Chunk(0, n))
                    sp.dma_start(lastd[:, :], dlast.partition_broadcast(P)).then_inc(lastd_in, 16)

                    def step(t, front, mid, rear, find, fetch, count):
                        if rear:
                            weights_beside(t + (-1))
                        if not (isinstance(t.i, int) and t.value() + 3 >= NC):
                            loads(t + 3)
                        if rear:
                            store(t + (-1))

                    steps(sp, step)
                    for s in range(2):
                        sp.wait_ge(o_out[s], 16 * (NC // 2))

                @block.gpsimd
                def _(pool):
                    def indices(c):
                        if not (isinstance(c.i, int) and c.value() < UN):
                            pool.wait_ge(q_full, c.value() - 3)
                            pool.sem_inc(pool_passed, 1)
                        nc.gpsimd.tensor_copy(idxs[:, c.slot(UN), :], idx_all[:, bass.ds(c.value() * 2 * TC, 2 * TC)])\
                            .then_inc(idx_made, 1)

                    def x_gathers(c):
                        s = c.slot(2)
                        if not (isinstance(c.i, int) and c.value() < 2):
                            pool.wait_ge(pair_full, front_use(c + (-2), X_) + 1)
                        pool.wait_ge(idx_made, c.value() + 1)
                        pool.sem_inc(pool_passed, 1)
                        for k in range(TC):
                            nc.gpsimd.indirect_dma_start(
                                out=gx[:, s, k, :], out_offset=None, in_=xg[:, :],
                                in_offset=bass.IndirectOffsetOnAxis(ap=idxs[:, c.slot(UN), k:k + 1], axis=0),
                            ).then_inc(x_in[s], 16)

                    def q_gathers(c, first, end):
                        s = c.slot(2)
                        if first == 0 and not (isinstance(c.i, int) and c.value() < 2):
                            pool.wait_ge(q_full, c.value() - 1)
                            pool.sem_inc(pool_passed, 1)
                        for k in range(first, end):
                            nc.gpsimd.indirect_dma_start(
                                out=gq[:, s, k, :], out_offset=None, in_=qtab[:, :],
                                in_offset=bass.IndirectOffsetOnAxis(ap=idxs[:, c.slot(UN), TC + k:TC + k + 1], axis=0),
                            ).then_inc(q_in[s], 16)

                    def weigh(c):
                        s, n = c.slot(2), c.value() + 1
                        pool.wait_ge(prob_done, n)
                        pool.wait_ge(v_done, n)
                        if not (isinstance(c.i, int) and c.value() < 2):
                            pool.wait_ge(n1_done, n - 2)
                        nc.gpsimd.tensor_tensor(pv[:, s, :], vv[:, s, :], prob[:, s, :], ALU.mult).then_inc(pv_done, 1)

                    def first_rest(c):
                        s = c.slot(2)
                        pool.wait_ge(zhi_done, 2 * c.value() + 1)
                        if not (isinstance(c.i, int) and c.value() < 2):
                            pool.wait_ge(tpv_full, c.value() - 1)
                        nc.gpsimd.tensor_tensor(zlo[:, s, 0, :], z[:, 0, :], zhi[:, s, 0, :].bitcast(fp32),
                                                ALU.subtract).then_inc(zlo0_done, 1)

                    indices(Chunk(0, 0))
                    x_gathers(Chunk(0, 0))
                    q_gathers(Chunk(0, 0), 0, TC)

                    def step(t, front, mid, rear, find, fetch, count):
                        ahead = not (isinstance(t.i, int) and t.value() + 2 >= NC)
                        if ahead:
                            indices(t + 2)
                            x_gathers(t + 2)
                        if rear:
                            weigh(t + (-1))
                        if ahead:
                            q_gathers(t + 2, 0, 2)
                        if front:
                            first_rest(t + 1)
                        if ahead:
                            q_gathers(t + 2, 2, TC)
                        if fetch is not None:
                            pool.wait_ge(row_slot, fetch + 1)
                            pool.sem_inc(pool_passed, 1)
                            nc.gpsimd.indirect_dma_start(
                                out=grow[:, :], out_offset=None, in_=dnow.rearrange("(r c) -> r c", c=SR),
                                in_offset=bass.IndirectOffsetOnAxis(ap=rslot[:, 0:1], axis=0)).then_inc(row_in, 16)

                    steps(pool, step)

                @block.scalar
                def _(act):
                    def take(t, k):
                        n = use(t, k)
                        act.wait_ge(pair_full, n + 1)
                        return pair[k % 2]

                    def old(c, by):
                        return not (isinstance(c.i, int) and c.value() < by)

                    def step(t, front, mid, rear, find, fetch, count):
                        c = t + 1
                        if front:
                            s = c.slot(2)
                            bank = take(t, X_)
                            if old(c, 2):
                                act.wait_ge(z_done, (c.value() - 1) * ST)
                            nc.scalar.activation(xd[:, s, :], bank[:, :], ACT.Copy).then_inc(pair_free, 1)

                        def hidden():
                            bank = take(t, HID)
                            if old(c, 1):
                                act.wait_ge(hidlo_done, c.value())
                            nc.scalar.activation(hid[:, :], bank[:, :], ACT.Relu, bias=b1c[:, 0:1]).then_inc(pair_free, 1)

                        def hid_first_part():
                            act.wait_ge(pair_free, use(t, HID) + 1)
                            nc.scalar.activation(hidhi[:, :], hid[:, :], ACT.Copy).then_inc(hidhi_done, 1)

                        if rear:
                            b = t + (-1)
                            s, n = b.slot(2), b.value() + 1
                            act.wait_ge(over_done, n)
                            if old(b, 1):
                                act.wait_ge(prob_done, n - 1)
                            nc.scalar.activation(below[:, :], over[:, s, :], ACT.Relu, scale=-1.0).then_inc(below_done, 1)
                            act.wait_ge(below_done, n)
                            if old(b, 2):
                                act.wait_ge(pv_done, n - 2)
                                act.wait_ge(prob2_in[s], 16 * b.turn(2))
                            nc.scalar.activation(prob[:, s, :], below[:, :], ACT.Exp, scale=-1.0).then_inc(prob_done, 1)
                            if front:
                                hidden()
                            if old(b, 1):
                                act.wait_ge(dec_done, n - 1)
                            nc.scalar.activation(rise[:, :], over[:, s, :], ACT.Relu).then_inc(rise_done, 1)
                            if front:
                                hid_first_part()
                            act.wait_ge(rise_done, n)
                            if old(b, 2):
                                act.wait_ge(n1_done, n - 2)
                                act.wait_ge(dec2_in[s], 16 * b.turn(2))
                            nc.scalar.activation(dec[:, s, :], rise[:, :], ACT.Exp, scale=-1.0).then_inc(dec_done, 1)
                        elif front:
                            hidden()
                            hid_first_part()
                        if front:
                            s = c.slot(2)
                            if old(c, 2):
                                act.wait_ge(tpv_full, c.value() - 1)
                            act.wait_ge(z_done, c.value() * ST + 3)
                            nc.scalar.activation(zhi[:, s, 0:3, :], z[:, 0:3, :], ACT.Copy).then_inc(zhi_done, 1)
                        if mid:
                            n = t.value() + 1
                            act.wait_ge(kq_done, n)
                            if old(t, 1):
                                act.wait_ge(a_full, n - 1)
                            nc.scalar.activation(kqhi[:, :], kq[:, :], ACT.Copy).then_inc(kqhi_done, 1)
                        if front:
                            s = c.slot(2)
                            act.wait_ge(z_done, c.value() * ST + ST)
                            nc.scalar.activation(zhi[:, s, 3:ST, :], z[:, 3:ST, :], ACT.Copy).then_inc(zhi_done, 1)
                            bank = take(t, WK)
                            if old(c, 2):
                                act.wait_ge(wkq_done, c.value() - 1)
                            nc.scalar.activation(wk[:, s, :], bank[:, :], ACT.Identity, bias=b2c[:, 0:1]).then_inc(pair_free, 1)
                        if count is not None:
                            act.wait_ge(row_in, count * 16 + 16)
                            act.sem_inc(act_passed, 1)
                            nc.scalar.activation(signs[:, :], grow[:, :], ACT.Sign, bias=nodeh[:, bass.ds(count, 1)],
                                                 scale=-1.0, accum_out=inrow[:, bass.ds(count, 1)]).then_inc(row_counted, 1)
                            act.wait_ge(row_counted, count + 1)
                        if find is not None:
                            at = bass.ds(find, 1)
                            act.sem_inc(act_passed, 1)
                            nc.scalar.activation(signs[:, :], lastd[:, :], ACT.Sign, bias=nodeh[:, at], scale=-1.0,
                                                 accum_out=rowc[:, at]).then_inc(row_found, 1)
                            act.wait_ge(row_found, find + 1)
                            act.sem_inc(act_passed, 1)
                            nc.scalar.activation(rslot[:, :], rowc[:, at], ACT.Copy, bias=SR / 2, scale=0.5).then_inc(row_slot, 1)
                        if front:
                            s = c.slot(2)
                            bank = take(t, WV)
                            if old(c, 2):
                                act.wait_ge(v_done, c.value() - 1)
                            nc.scalar.activation(wv[:, s, :], bank[:, :], ACT.Identity, bias=b2c[:, 1:2]).then_inc(pair_free, 1)
                        if mid:
                            if old(t, 2):
                                act.wait_ge(n2_done, t.value() - 1)
                            act.wait_ge(n_in[t.slot(UN)], 16 * (t.turn(UN) + 1))
                            nc.scalar.activation(d2[0:D, t.slot(2), :], nm[0:D, t.slot(UN), :], ACT.Relu, bias=1.0)\
                                .then_inc(mask_done, 1)
                        if rear:
                            b = t + (-1)
                            s = b.slot(2)
                            if old(b, 2):
                                act.wait_ge(o_out[s], 16 * b.turn(2))
                            for half, k in enumerate((ROWA, ROWB)):
                                bank = take(t, k)
                                nc.scalar.activation(ot[:, s, 2 * half:2 * half + 2, :],
                                                     bank[:, :].rearrange("p (t w) -> p t w", t=2)[:, :, 0:RW],
                                                     ACT.Copy).then_inc(pair_free, 1)
                    act.wait_ge(lastd_in, 16)
                    steps(act, step)

                @block.vector
                def _(dve):
                    v = nc.vector
                    v.memset(mprev[:, 0, 0:1], -BIG).then_inc(zeroed, 1)
                    v.memset(n1[:, 1, CH - 1:CH], 0.0).then_inc(zeroed, 1)
                    v.memset(n2[:, 1, CH - 1:CH], 0.0).then_inc(zeroed, 1)
                    dve.wait_ge(zeroed, 3)

                    def old(c, by):
                        return not (isinstance(c.i, int) and c.value() < by)

                    def step(t, front, mid, rear, find, fetch, count):
                        if front:
                            c = t + 1
                            s = c.slot(2)
                            dve.wait_ge(pair_free, front_use(c, X_) + 1)
                            for j in range(ST):
                                dve.wait_ge(shb_full, c.value() * ST + j + 1)
                                if j == 0 and old(c, 1):
                                    dve.wait_ge(zlo_done, c.value() * 3)
                                    dve.wait_ge(zlo0_done, c.value())
                                v.tensor_tensor(z[:, j, :], sbank[(s + j) % 2][:, :], xd[:, s, :],
                                                ALU.mult).then_inc(z_done, 1)
                                if j == 3:
                                    dve.wait_ge(hidhi_done, c.value() + 1)
                                    if old(c, 1):
                                        dve.wait_ge(pair_free, front_use(c + (-1), WV) + 1)
                                    v.tensor_tensor(hidlo[:, :], hid[:, :], hidhi[:, :].bitcast(fp32),
                                                    ALU.subtract).then_inc(hidlo_done, 1)
                        if rear:
                            b = t + (-1)
                            s, n = b.slot(2), b.value() + 1
                            dve.wait_ge(pv_done, n)
                            dve.wait_ge(dec_done, n)
                            if old(b, 1):
                                dve.wait_ge(n2_done, n - 1)
                            if old(b, 2):
                                dve.wait_ge(pair_full, use(t + (-2), ROWB) + 1)
                            v.tensor_tensor_scan(n1[:, s, :], dec[:, s, :], pv[:, s, :], n1[:, 1 - s, CH - 1:CH],
                                                 ALU.mult, ALU.add).then_inc(n1_done, 1)
                        if mid:
                            s, n = t.slot(2), t.value() + 1
                            dve.wait_ge(wkq_done, n)
                            dve.wait_ge(tpk_full, n)
                            if old(t, 1):
                                dve.wait_ge(kqlo_done, n - 1)
                            v.tensor_tensor(kq[:, :], tpk[:, :], wkq[:, s, :], ALU.mult).then_inc(kq_done, 1)
                        if front:
                            c = t + 1
                            s, n = c.slot(2), c.value() + 1
                            dve.wait_ge(zhi_done, 2 * n - 1)
                            if old(c, 2):
                                dve.wait_ge(tpv_full, n - 2)
                            v.tensor_tensor(zlo[:, s, 1:3, :], z[:, 1:3, :], zhi[:, s, 1:3, :].bitcast(fp32),
                                            ALU.subtract).then_inc(zlo_done, 1)
                        if rear:
                            b = t + (-1)
                            s, n = b.slot(2), b.value() + 1
                            dve.wait_ge(mask_done, n)
                            dve.wait_ge(prob2_in[s], 16 * (b.turn(2) + 1))
                            dve.wait_ge(dec2_in[s], 16 * (b.turn(2) + 1))
                            dve.wait_ge(e_in[b.slot(UN)], 16 * (b.turn(UN) + 1))
                            v.tensor_tensor_scan(n2[:, s, :], d2[:, s, :], v2[:, b.slot(UN), :],
                                                 n2[:, 1 - s, CH - 1:CH], ALU.mult, ALU.add).then_inc(n2_done, 1)
                        if mid:
                            s, n = t.slot(2), t.value() + 1
                            dve.wait_ge(kqhi_done, n)
                            if old(t, 1):
                                dve.wait_ge(a_full, n - 1)
                            v.tensor_tensor(kqlo[:, :], kq[:, :], kqhi[:, :].bitcast(fp32), ALU.subtract).then_inc(kqlo_done, 1)
                        if front:
                            c = t + 1
                            s, n = c.slot(2), c.value() + 1
                            dve.wait_ge(zhi_done, 2 * n)
                            v.tensor_tensor(zlo[:, s, 3:ST - 1, :], z[:, 3:ST - 1, :], zhi[:, s, 3:ST - 1, :].bitcast(fp32),
                                            ALU.subtract).then_inc(zlo_done, 1)
                            v.tensor_tensor(zhi[D:P, s, ST - 1, :], z[D:P, ST - 1, :],
                                            zhi[D:P, s, ST - 1, :].bitcast(fp32), ALU.subtract).then_inc(zlo_done, 1)
                        if mid:
                            s, n = t.slot(2), t.value() + 1
                            dve.wait_ge(tpv_full, n)
                            dve.wait_ge(pair_free, front_use(t, WV) + 1)
                            v.tensor_tensor(vv[:, s, :], tpv[:, :], wv[:, s, :], ALU.mult).then_inc(v_done, 1)
                            dve.wait_ge(a_full, n)
                            dve.wait_ge(n_in[t.slot(UN)], 16 * (t.turn(UN) + 1))
                            if old(t, 1):
                                dve.wait_ge(mcol_done, n - 1)
                            v.tensor_tensor_scan(mprev[:, s, 1:CH], abank[:, 0:CH - 1], nm[:, t.slot(UN), 1:CH], mprev[:, s, 0:1],
                                                 ALU.max, ALU.add).then_inc(m_done, 1)
                            dve.wait_ge(m_done, n)
                            if old(t, 2):
                                dve.wait_ge(rise_done, n - 2)
                            v.tensor_tensor(over[:, s, :], abank[:, :], mprev[:, s, :], ALU.subtract).then_inc(over_done, 1)
                            if front:
                                dve.wait_ge(n_in[(t + 1).slot(UN)], 16 * ((t + 1).turn(UN) + 1))
                                if old(t, 1):
                                    dve.wait_ge(over_done, n - 1)
                                v.scalar_tensor_tensor(out=mprev[:, 1 - s, 0:1], in0=abank[:, CH - 1:CH],
                                                       scalar=mprev[:, s, CH - 1:CH],
                                                       in1=nm[:, (t + 1).slot(UN), 0:1], op0=ALU.max,
                                                       op1=ALU.add).then_inc(mcol_done, 1)
                        if front:
                            c = t + 1
                            s, n = c.slot(2), c.value() + 1
                            dve.wait_ge(q_full, n)
                            dve.wait_ge(pair_free, front_use(c, WK) + 1)
                            if old(c, 2):
                                dve.wait_ge(kq_done, n - 2)
                            v.tensor_tensor(wkq[:, s, :], qbank[:, :], wk[:, s, :], ALU.mult).then_inc(wkq_done, 1)

                    steps(dve, step)

                @block.tensor
                def _(pe):
                    def take(t, k):
                        n = use(t, k)
                        if not (isinstance(t.i, int) and n < 2):
                            pe.wait_ge(pair_free, n - 1)
                        return pair[k % 2]

                    def old(c, by):
                        return not (isinstance(c.i, int) and c.value() < by)

                    def step(t, front, mid, rear, find, fetch, count):
                        c = t + 1
                        cs = c.slot(2)

                        def spread(j):
                            n = c.value() * ST + j
                            if not (isinstance(c.i, int) and n < 2):
                                pe.wait_ge(z_done, n - 1)
                            nc.tensor.matmul(sbank[(cs + j) % 2][:, :], bs[:, j, :], hp[:, c.slot(UN), :],
                                             start=True, stop=True).then_inc(shb_full, 1)

                        def product(out, o, s, j):
                            hi, lo = chi[:, j, o:o + O], clo[:, j, o:o + O]
                            nc.tensor.matmul(out[:, :], hi, zhi[:, s, j, :], start=(j == 0), stop=False)
                            if j < ST - 1:
                                nc.tensor.matmul(out[:, :], hi, zlo[:, s, j, :], start=False, stop=False)
                                return nc.tensor.matmul(out[:, :], lo, zhi[:, s, j, :], start=False, stop=False)
                            return nc.tensor.matmul(out[:, :], lo[0:D, :], zhi[0:D, s, j, :], start=False, stop=True)

                        def by_hid(bank, k):
                            nc.tensor.matmul(bank[:, :], w2hi[:, k, :], hidhi[:, :], start=True, stop=False)
                            nc.tensor.matmul(bank[:, :], w2hi[:, k, :], hidlo[:, :], start=False, stop=False)
                            return nc.tensor.matmul(bank[:, :], w2lo[:, k, :], hidhi[:, :], start=False, stop=True)

                        if front:
                            bank = take(t, X_)
                            pe.wait_ge(x_in[cs], 16 * TC * (c.turn(2) + 1))
                            for k in range(TC):
                                mm = nc.tensor.transpose(bank[:, k * P:(k + 1) * P], gx[:, cs, k, :], idn[:, :])
                            mm.then_inc(pair_full, 1)
                            pe.wait_ge(h_in[c.slot(UN)], 16 * (c.turn(UN) + 1))
                            spread(0)
                            spread(1)
                            bank = take(t, HID)
                            pe.wait_ge(e_in[c.slot(UN)], 16 * (c.turn(UN) + 1))
                            nc.tensor.matmul(bank[:, :], w1[:, :], v2[0:D, c.slot(UN), :],
                                             start=True, stop=True).then_inc(pair_full, 1)
                        if mid:
                            s, n = t.slot(2), t.value() + 1
                            pe.wait_ge(zlo_done, n * 3)
                            pe.wait_ge(zlo0_done, n)
                            if old(t, 1):
                                pe.wait_ge(kq_done, n - 1)
                            for j in range(ST):
                                mm = product(tpk, 0, s, j)
                                if front and j < 3:
                                    spread(j + 2)
                            mm.then_inc(tpk_full, 1)
                        elif front:
                            for j in range(2, ST):
                                spread(j)
                        if front:
                            bank = take(t, WK)
                            pe.wait_ge(hidlo_done, c.value() + 1)
                            by_hid(bank, 0).then_inc(pair_full, 1)
                            bank = take(t, WV)
                            by_hid(bank, 1).then_inc(pair_full, 1)
                        if mid:
                            if old(t, 1):
                                pe.wait_ge(v_done, n - 1)
                            for j in range(ST):
                                mm = product(tpv, O, s, j)
                            mm.then_inc(tpv_full, 1)
                        if mid:
                            n = t.value() + 1
                            pe.wait_ge(kqlo_done, n)
                            if old(t, 1):
                                pe.wait_ge(mcol_done, n - 1)
                            nc.tensor.matmul(abank[:, :], hs[:, :], kqhi[:, :], start=True, stop=False)
                            nc.tensor.matmul(abank[:, :], hs[:, :], kqlo[:, :], start=False, stop=True).then_inc(a_full, 1)
                        if rear:
                            b = t + (-1)
                            s, n = b.slot(2), b.value() + 1
                            pe.wait_ge(n2_done, n)
                            for half, k in enumerate((ROWA, ROWB)):
                                bank = take(t, k)
                                for m in range(2):
                                    e0 = (2 * half + m) * P
                                    nc.tensor.transpose(bank[:, 256 * m:256 * m + O], n1[:, s, e0:e0 + P], idn[:, :])
                                    mm = nc.tensor.transpose(bank[:, 256 * m + O:256 * m + RW], n2[:, s, e0:e0 + P],
                                                             idn[0:D + H, 0:D + H])
                                mm.then_inc(pair_full, 1)
                        if front:
                            pe.wait_ge(q_in[cs], 16 * TC * (c.turn(2) + 1))
                            if old(c, 1):
                                pe.wait_ge(wkq_done, c.value())
                            for k in range(TC):
                                mm = nc.tensor.transpose(qbank[:, k * P:(k + 1) * P], gq[:, cs, k, :], idn[:, :])
                            mm.then_inc(q_full, 1)

                    steps(pe, step)

        with ExitStack() as fin:
            fs = lambda name, shape, dt=fp32: fin.enter_context(nc.sbuf_tensor(name, shape, dt))
            xp = fs("xp", [P, HC])
            o0 = fs("o0", [P, HC])
            eh = fs("eh", [P, HC])
            tmpc = fs("tmpc", [P, 4, NT + 1])
            lasti = fs("lasti", [P, 2, NT // 2], i32)
            some = fs("some", [P, 2, NT // 2])
            inv = fs("inv", [P, 2, NT // 2])
            st = fs("st", [P, 10])
            parts = fs("parts", [P, 5])

            each = lambda name, n: [sem(f"{name}{i}") for i in range(n)]
            g_l, y_s = each("rows_gathered", G), each("y_stored", GN)
            xp_in, last_made, counts_made = sem("xp_in"), sem("last_made"), sem("counts_made")
            av_zero, eh_made, eh_copied = sem("av_zero"), sem("eh_made"), sem("eh_copied")
            lslot_made, den_ok, rec_made, rec_some, up_made, av_made = (
                sem("lslot_made"), sem("den_ok"), sem("rec_made"), sem("rec_some"), sem("up_made"), sem("av_made"))
            upT_made, upT_copied, avT_made, avT_copied, o0_made, o0_copied = (
                sem("upT_made"), sem("upT_copied"), sem("avT_made"), sem("avT_copied"), sem("o0_made"), sem("o0_copied"))
            st_d, st_a, st_pe = sem("stats_dve"), sem("stats_act"), sem("stats_pe")
            SS = {k: sem(f"{k}_made") for k in ("r", "y", "mean", "dd", "sq", "var", "lg", "rs", "x1", "z0", "s0", "h0", "z1",
                                                "h1", "z2", "y2", "mean2", "dd2", "sq2", "var2", "lg2", "rs2", "o")}

            with ExitStack() as fin1:
                f1 = lambda name, shape, dt=fp32: fin1.enter_context(nc.sbuf_tensor(name, shape, dt))
                lslot = f1("lslot", [P, G, TC], i32)
                gr = f1("gr", [P, G, TC, RW])
                rec = f1("rec", [P, G, 3, TC * H])
                up = f1("up", [P, G, TC, O])
                av = f1("av", [P, G, 2, 2, D])
                upT = f1("upT", [P, G, CH])
                avT = f1("avT", [P, G, CH // 2])
                W1C = 2 * P

                def cols(i, j):
                    return bass.ds(i * G * W1C + j * W1C, W1C)

                def tiles(i, j):
                    return bass.ds(i * G * 2 + j * 2, 2)

                with nc.Block() as block:
                    @block.sync
                    def _(sp):
                        sp.dma_start(xp[:, :], xP).then_inc(xp_in, 16)
                        sp.wait_ge(xp_in, 16)

                    @block.gpsimd
                    def _(pool):
                        pool.wait_ge(last_made, 1)

                        def slots(i, j):
                            if past(i):
                                pool.wait_ge(av_made, (i - 1) * G + (j + 1))
                                pool.sem_inc(pool_passed, 1)
                            nc.gpsimd.tensor_copy(lslot[:, j, :].rearrange("p (h t) -> p h t", h=2),
                                                  lasti[:, :, tiles(i, j)]).then_inc(lslot_made, 1)

                        def turn(i):
                            slots(i, 0)
                            for j in range(G):
                                if j + 1 < G:
                                    slots(i, j + 1)
                                pool.wait_ge(lslot_made, i * G + (j + 1))
                                pool.sem_inc(pool_passed, 1)
                                for k in range(TC):
                                    nc.gpsimd.indirect_dma_start(
                                        out=gr[:, j, k, :], out_offset=None, in_=rows[:, :],
                                        in_offset=bass.IndirectOffsetOnAxis(ap=lslot[:, j, k:k + 1], axis=0),
                                    ).then_inc(g_l[j], 16)

                        turns_of(pool, NB // G, turn)

                    @block.tensor
                    def _(pe):
                        t = nc.tensor
                        pe.wait_ge(xp_in, 16)

                        def turn(i):
                            for j in range(G):
                                pe.wait_ge(up_made, i * G + (j + 1))
                                if past(i):
                                    pe.wait_ge(o0_copied, i * G)
                                for k in range(TC):
                                    mm = t.transpose(banks[j][:, k * P:(k + 1) * P], up[:, j, k, :], idn[:, :])
                                mm.then_inc(upT_made, 1)
                            for j in range(G):
                                pe.wait_ge(upT_copied, i * G + (j + 1))
                                pe.wait_ge(av_made, i * G + (j + 1))
                                for k in range(2):
                                    mm = t.transpose(banks[j][:, k * P:(k + 1) * P],
                                                     av[:, j, k, :, :].rearrange("p h d -> p (h d)"), idn[:, :])
                                mm.then_inc(avT_made, 1)
                            for j in range(G):
                                pe.wait_ge(avT_copied, i * G + (j + 1))
                                t.matmul(banks[j][:, W1C:2 * W1C], m0e[:, :], avT[:, j, :], start=True, stop=True)\
                                    .then_inc(eh_made, 1)
                            for j in range(G):
                                pe.wait_ge(eh_copied, i * G + (j + 1))
                                out0 = banks[j][:, 0:W1C]
                                t.matmul(out0, wself[:, :], xp[:, cols(i, j)], start=True, stop=False)
                                t.matmul(out0, wout[:, 0, :], upT[:, j, 0:W1C], start=False, stop=False)
                                t.matmul(out0, wout[:, 1, :], upT[:, j, W1C:2 * W1C], start=False, stop=True)\
                                    .then_inc(o0_made, 1)

                        turns_of(pe, NB // G, turn)

                    @block.scalar
                    def _(act):
                        f = nc.scalar.activation

                        def turn(i):
                            for j in range(G):
                                act.wait_ge(upT_made, i * G + (j + 1))
                                f(upT[:, j, :], banks[j][:, :], ACT.Copy).then_inc(upT_copied, 1)
                            for j in range(G):
                                act.wait_ge(avT_made, i * G + (j + 1))
                                f(avT[:, j, :], banks[j][:, 0:W1C], ACT.Copy).then_inc(avT_copied, 1)
                            for j in range(G):
                                act.wait_ge(eh_made, i * G + (j + 1))
                                f(eh[:, cols(i, j)], banks[j][:, W1C:2 * W1C], ACT.Identity, bias=mb[:, 0:1])\
                                    .then_inc(eh_copied, 1)
                            for j in range(G):
                                act.wait_ge(o0_made, i * G + (j + 1))
                                f(o0[:, cols(i, j)], banks[j][:, 0:W1C], ACT.Copy).then_inc(o0_copied, 1)

                        turns_of(act, NB // G, turn)

                    @block.vector
                    def _(dve):
                        v = nc.vector
                        flat = lambda a: a[:, :, :].rearrange("p h t -> p (h t)")
                        v.tensor_scalar(tmpc[:, 0, :], rowc[:, :], SR / 2.0, SR * SR / 2.0 + SR / 2.0, ALU.mult, ALU.add)\
                            .then_inc(counts_made, 1)
                        dve.wait_ge(counts_made, 1)
                        v.scalar_tensor_tensor(out=tmpc[:, 1, :], in0=inrow[:, :], scalar=0.5, in1=tmpc[:, 0, :],
                                               op0=ALU.mult, op1=ALU.add).then_inc(counts_made, 1)
                        dve.wait_ge(counts_made, 2)
                        v.tensor_scalar(tmpc[:, 2, 0:NT], tmpc[:, 1, 1:NT + 1], -1.0, 0.0, ALU.add, ALU.max)\
                            .then_inc(counts_made, 1)
                        dve.wait_ge(counts_made, 3)
                        v.tensor_copy(flat(lasti), tmpc[:, 2, 0:NT]).then_inc(last_made, 1)
                        v.tensor_tensor(flat(inv), tmpc[:, 1, 1:NT + 1], tmpc[:, 1, 0:NT], ALU.subtract).then_inc(counts_made, 1)
                        dve.wait_ge(counts_made, 4)
                        v.tensor_scalar(flat(some), flat(inv), 1.0, None, ALU.min).then_inc(counts_made, 1)
                        v.tensor_scalar(tmpc[:, 3, 0:NT], flat(inv), 1.0, None, ALU.max).then_inc(counts_made, 1)
                        dve.wait_ge(counts_made, 6)
                        v.reciprocal(tmpc[:, 0, 0:NT], tmpc[:, 3, 0:NT]).then_inc(counts_made, 1)
                        dve.wait_ge(counts_made, 7)
                        v.tensor_tensor(flat(inv), tmpc[:, 0, 0:NT], flat(some), ALU.mult).then_inc(counts_made, 1)
                        dve.wait_ge(counts_made, 8)

                        def turn(i):
                            for j in range(G):
                                n = i * G + (j + 1)
                                dve.wait_ge(g_l[j], i * 16 * TC + 16 * TC)
                                rv = [rec[:, j, q, :].rearrange("p (t h) -> p t h", h=H) for q in range(3)]
                                four = lambda a: a.rearrange("p (a t) h -> p a t h", a=2)
                                v.tensor_scalar(rv[0], gr[:, j, :, O + D:RW], 1e-16, None, ALU.add).then_inc(den_ok, 1)
                                dve.wait_ge(den_ok, n)
                                v.reciprocal(rv[1], rv[0]).then_inc(rec_made, 1)
                                dve.wait_ge(rec_made, n)
                                v.tensor_tensor(four(rv[2]), four(rv[1]),
                                                some[:, :, tiles(i, j)].unsqueeze(3).broadcast_to([P, 2, 2, H]),
                                                ALU.mult).then_inc(rec_some, 1)
                                dve.wait_ge(rec_some, n)
                                if past(i):
                                    dve.wait_ge(avT_made, i * G)
                                v.tensor_tensor(up[:, j, :, :].rearrange("p t (d h) -> p t d h", h=H),
                                                gr[:, j, :, 0:O].rearrange("p t (d h) -> p t d h", h=H),
                                                rv[2].unsqueeze(2).broadcast_to([P, TC, DH, H]), ALU.mult).then_inc(up_made, 1)
                                v.tensor_tensor(av[:, j, :, :, :].rearrange("p t h d -> p h t d"),
                                                gr[:, j, :, O:O + D].rearrange("p (h t) d -> p h t d", h=2),
                                                inv[:, :, tiles(i, j)].unsqueeze(3).broadcast_to([P, 2, 2, D]),
                                                ALU.mult).then_inc(av_made, 1)

                        turns_of(dve, NB // G, turn)

            with ExitStack() as fin2:
                f2 = lambda name, shape, dt=fp32: fin2.enter_context(nc.sbuf_tensor(name, shape, dt))
                junk = f2("junk", [P, 10 * ROWS_OK], bf16)
                work = {k: f2(f"{k}_", [P, GN, CN]) for k in ("r", "y", "dd", "sq", "lg", "rs", "x1")}
                work |= {"y2": work["r"], "h1": work["y"], "h0": work["dd"]}
                W = lambda k, j: work[k][:, j, :]
                bank_of = lambda j: banks[j][:, 0:CN]

                def ncols(i, j):
                    return bass.ds(i * GN * CN + j * CN, CN)

                with nc.Block() as block:
                    @block.sync
                    def _(sp):
                        def turn(i):
                            for j in range(GN):
                                sp.wait_ge(SS["o"], i * GN + (j + 1))
                                sp.dma_start(out[:, ncols(i, j)], W("sq", j)).then_inc(y_s[j], 16)

                        turns_of(sp, NN // GN, turn)
                        for j in range(GN):
                            sp.wait_ge(y_s[j], 16 * (NN // GN))

                    @block.tensor
                    def _(pe):
                        t = nc.tensor
                        for k in range(2):
                            pe.wait_ge(st_d, 1 + 2 * k)
                            t.matmul(banks[k][:, 0:2], fold[:, :], st[:, 2 * k:2 * k + 2], start=True, stop=True).then_inc(st_pe, 1)

                        def product(name, lhsT, after, src, i):
                            for j in range(GN):
                                pe.wait_ge(SS[after], i * GN + (j + 1))
                                t.matmul(bank_of(j), lhsT[:, :], W(src, j), start=True, stop=True).then_inc(SS[name], 1)

                        def turn(i):
                            product("mean", mn, "y", "y", i)
                            product("var", mn, "sq", "sq", i)
                            product("z0", m0x, "x1", "x1", i)
                            product("z1", m1, "h0", "h0", i)
                            product("z2", m2, "h1", "h1", i)
                            product("mean2", mn, "y2", "y2", i)
                            product("var2", mn, "sq2", "sq", i)

                        turns_of(pe, NN // GN, turn)

                    @block.scalar
                    def _(act):
                        f = nc.scalar.activation
                        act.wait_ge(st_d, 2)
                        ov = o0[:, :].rearrange("d (t p) -> d t p", p=P)
                        for q in range(5):
                            if q:
                                act.wait_ge(st_a, q)
                            f(junk[:, :].rearrange("d (t p) -> d t p", p=ROWS_OK), ov[:, 10 * q:10 * q + 10, 0:ROWS_OK],
                              ACT.Square, bias=st[:, 4:5], accum_out=parts[:, q:q + 1]).then_inc(st_a, 1)
                        act.wait_ge(st_pe, 2)
                        f(st[:, 5:6], banks[1][:, 0:1], ACT.Ln, bias=epsc[:, 0:1], scale=1.0 / N).then_inc(st_a, 1)
                        act.wait_ge(st_a, 6)
                        f(st[:, 6:7], st[:, 5:6], ACT.Exp, scale=-0.5).then_inc(st_a, 1)

                        def each_block(name, after, fn, i):
                            for j in range(GN):
                                act.wait_ge(SS[after], i * GN + (j + 1))
                                fn(j).then_inc(SS[name], 1)

                        act.wait_ge(st_d, 6)

                        def turn(i):
                            for j in range(GN):
                                if past(i):
                                    act.wait_ge(SS["o"], i * GN)
                                f(W("r", j), xp[:, ncols(i, j)], ACT.Identity, bias=st[:, 9:10]).then_inc(SS["r"], 1)
                            for j in range(GN):
                                if past(i):
                                    act.wait_ge(y_s[j], i * 16)
                                act.wait_ge(SS["dd"], i * GN + (j + 1))
                                f(W("sq", j), W("dd", j), ACT.Square).then_inc(SS["sq"], 1)
                            each_block("lg", "var", lambda j: f(W("lg", j), bank_of(j), ACT.Ln, bias=epsc[:, 0:1]), i)
                            each_block("rs", "lg", lambda j: f(W("rs", j), W("lg", j), ACT.Exp, scale=-0.5), i)
                            each_block("h0", "s0", lambda j: f(W("h0", j), W("r", j), ACT.Relu), i)
                            each_block("h1", "z1", lambda j: f(W("h1", j), bank_of(j), ACT.Relu, bias=mb[:, 1:2]), i)
                            each_block("sq2", "dd2", lambda j: f(W("sq", j), W("dd", j), ACT.Square), i)
                            each_block("lg2", "var2", lambda j: f(W("lg", j), bank_of(j), ACT.Ln, bias=epsc[:, 0:1]), i)
                            each_block("rs2", "lg2", lambda j: f(W("rs", j), W("lg", j), ACT.Exp, scale=-0.5), i)

                        turns_of(act, NN // GN, turn)

                    @block.vector
                    def _(dve):
                        v = nc.vector
                        v.memset(st[:, :], 0.0).then_inc(av_zero, 1)
                        dve.wait_ge(av_zero, 1)
                        ov = o0[:, :].rearrange("d (t p) -> d t p", p=P)[:, :, 0:ROWS_OK]
                        v.tensor_reduce(st[:, 0:1], ov, AX.XY, ALU.add).then_inc(st_d, 1)
                        dve.wait_ge(st_pe, 1)
                        v.tensor_scalar(st[:, 4:5], banks[0][:, 0:1], -1.0 / N, None, ALU.mult).then_inc(st_d, 1)
                        dve.wait_ge(st_a, 5)
                        v.tensor_reduce(st[:, 2:3], parts[:, :], AX.X, ALU.add).then_inc(st_d, 1)
                        dve.wait_ge(st_a, 7)
                        v.tensor_tensor(st[:, 7:8], st[:, 6:7], gb[:, 0:1], ALU.mult).then_inc(st_d, 1)
                        dve.wait_ge(st_d, 4)
                        v.tensor_tensor(st[:, 8:9], st[:, 7:8], st[:, 4:5], ALU.mult).then_inc(st_d, 1)
                        dve.wait_ge(st_d, 5)
                        v.tensor_tensor(st[:, 9:10], st[:, 8:9], gb[:, 1:2], ALU.add).then_inc(st_d, 1)

                        def each_block(name, after, fn, i):
                            for j in range(GN):
                                dve.wait_ge(SS[after], i * GN + (j + 1))
                                fn(j).then_inc(SS[name], 1)

                        def turn(i):
                            each_block("y", "r", lambda j: v.scalar_tensor_tensor(
                                out=W("y", j), in0=o0[:, ncols(i, j)], scalar=st[:, 7:8], in1=W("r", j),
                                op0=ALU.mult, op1=ALU.add), i)
                            each_block("dd", "mean", lambda j: v.tensor_tensor(W("dd", j), W("y", j), bank_of(j), ALU.subtract), i)
                            each_block("x1", "rs", lambda j: v.tensor_tensor(W("x1", j), W("dd", j), W("rs", j), ALU.mult), i)
                            each_block("s0", "z0", lambda j: v.tensor_tensor(W("r", j), bank_of(j), eh[:, ncols(i, j)], ALU.add), i)
                            each_block("y2", "z2", lambda j: v.scalar_tensor_tensor(
                                out=W("y2", j), in0=bank_of(j), scalar=mb[:, 2:3], in1=W("x1", j),
                                op0=ALU.add, op1=ALU.add), i)
                            each_block("dd2", "mean2", lambda j: v.tensor_tensor(W("dd", j), W("y2", j), bank_of(j),
                                                                                 ALU.subtract), i)
                            each_block("o", "rs2", lambda j: v.tensor_tensor(W("sq", j), W("dd", j), W("rs", j), ALU.mult), i)

                        turns_of(dve, NN // GN, turn)


def kernel(**inputs):
    import numpy as np
    import concourse.bacc as bacc
    import ml_dtypes
    from concourse.bass_utils import run_bass_kernel_spmd

    g = {k: np.asarray(v) for k, v in inputs.items()}
    hd = lambda w: np.ascontiguousarray(w.reshape(w.shape[:-1] + (H, DH)).swapaxes(-1, -2).reshape(w.shape))
    pad_e = lambda v, fill: np.concatenate([v, np.full(EP - E, fill, v.dtype)])
    tiles = lambda v: pad_e(v, 0).reshape(NC, TC, P).transpose(2, 0, 1)
    col = lambda v: v.reshape(-1, 1)
    none = np.zeros((D, D), np.float32)
    twice = lambda w: np.block([[w, none], [none, w]])
    both_rows = lambda *v: np.stack([np.concatenate([a, a]) for a in v], axis=1)

    x = g["x"]
    xT = np.zeros((D, NT, P), x.dtype)
    xT[:, :, :ROWS_OK] = x.reshape(ROWS_OK, NT, D).transpose(2, 1, 0)
    both = np.concatenate([hd(g["L0_gnn_Cqk"]), hd(g["L0_gnn_Cv"])], axis=-1)
    ctp = np.zeros((2, D, ST, 2 * O), both.dtype)
    for s in range(S):
        ctp[s % 2, :, s // 2] = both[:, s]
    ctp[1, :, ST - 1] = both[:, S - 1]
    shT = np.zeros((S, EP), np.float32)
    shT[:, :E] = g["edge_attr_9"].T
    eT = np.zeros((D, EP), np.float32)
    eT[:, :E] = g["edge_attr_64"].T

    bsel = np.zeros((3, S, ST, P), np.float32)
    for s in range(S):
        bsel[:, s, s // 2, (s % 2) * D:(s % 2 + 1) * D] = 1
    bsel[:, S - 1, ST - 1, :] = 1
    hsel = (np.arange(P)[:, None] % H == np.arange(P)[None, :] % H).astype(np.float32)

    wout = g["L0_gnn_W_out"].reshape(H, DH, D).transpose(1, 0, 2).reshape(O, D)
    arrays = {
        "xg": np.concatenate([x, x], axis=1), "xT": xT.reshape(D, NP),
        "idx": np.concatenate([tiles(g["src"]), tiles(g["dst"])], axis=2).reshape(P, NC * 2 * TC),
        "dnow": pad_e(g["dst"], NP), "dbefore": np.concatenate([np.full(1, -1, np.int32), pad_e(g["dst"], NP)[:-1]]),
        "dlast": pad_e(g["dst"], NP)[SR - 1::SR], "shT": shT, "eT": eT, "Wq": hd(g["L0_gnn_Wq"]), "Ctp": ctp.reshape(P, ST, 2 * O),
        "W1": np.concatenate([g["L0_gnn_k_w1"], g["L0_gnn_v_w1"]], axis=1),
        "b1": col(np.concatenate([g["L0_gnn_k_b1"], g["L0_gnn_v_b1"]])),
        "Wk2": hd(g["L0_gnn_k_w2"]), "Wv2": hd(g["L0_gnn_v_w2"]),
        "b2": np.stack([hd(g["L0_gnn_k_b2"]), hd(g["L0_gnn_v_b2"])], axis=1),
        "Wout": np.stack([np.concatenate([wout, np.zeros_like(wout)], axis=1), np.concatenate([np.zeros_like(wout), wout], axis=1)], axis=1),
        "Wself": twice(g["L0_gnn_W_self"]), "gamma_beta": both_rows(g["L0_gnn_gamma"], g["L0_gnn_beta"]),
        "M0e": twice(g["L1_gnn_W0"][:D]), "M0x": twice(g["L1_gnn_W0"][D:]), "M1": twice(g["L1_gnn_W1"]),
        "M2": twice(g["L1_gnn_W2"]), "mbias": both_rows(g["L1_gnn_b0"], g["L1_gnn_b1"], g["L1_gnn_b2"]),
        "bsel": bsel.reshape(3 * S, ST, P).astype(ml_dtypes.bfloat16), "hsel": hsel,
        "ident": np.eye(P, dtype=np.float32), "mean64": twice(np.full((D, D), 1.0 / D, np.float32)),
        "halves": np.tile(np.eye(D, dtype=np.float32), (2, 2)),
        "xP": xT.reshape(D, 2, HC).transpose(1, 0, 2).reshape(P, HC),
    }
    arrays = {f"in_{k}": np.ascontiguousarray(v) for k, v in arrays.items()}
    nc = bacc.Bacc("TRN2", target_bir_lowering=False, num_devices=1)
    args = [nc.dram_tensor(k, v.shape, mybir.dt.from_np(v.dtype), kind="ExternalInput").ap() for k, v in arrays.items()]
    res = nc.dram_tensor("out_y", (P, HC), fp32, kind="ExternalOutput").ap()
    gnn_kernel(nc, *args, res)
    r = run_bass_kernel_spmd(nc, [arrays], core_ids=[0])
    y = r.results[0]["out_y"].reshape(2, D, HC).transpose(1, 0, 2).reshape(D, NT, P)[:, :, :ROWS_OK]
    return np.ascontiguousarray(y.transpose(2, 1, 0).reshape(N, D))
```
